# Optimizing a Trainium2 kernel written in Bass

```python
import numpy as np
import jax
import jax.numpy as jnp

def _softmax(x, axis=-1):
    return jax.nn.softmax(x, axis=axis)

def _gelu(x):
    return jax.nn.gelu(x, approximate=True)

def _silu(x):
    return jax.nn.silu(x)

def _sigmoid(x):
    return jax.nn.sigmoid(x)

def _layernorm(x, axis=-1, eps=1e-05):
    m = jnp.mean(x, axis=axis, keepdims=True)
    v = jnp.var(x, axis=axis, keepdims=True)
    return (x - m) / jnp.sqrt(v + eps)

def _scatter_add(tgt, idx, src, axis=0):
    return tgt.at[idx].add(src)

def _segment_sum(src, seg, n):
    return jax.ops.segment_sum(src, seg, n)
kernel_name = 'mk_gnn_resnorm_d4_gnn_r8_991eb9'

def setup_inputs(seed: int=0):
    np.random.seed(seed)
    _w = jnp.asarray

    def _rec_inputs():
        import jax
        import jax.numpy as jnp
        _gk = jax.random.key(seed)
        x = -0.0003713 + 1 * jax.random.normal(jax.random.fold_in(_gk, 1), (12500, 128), jnp.float32)
        src = jax.random.randint(jax.random.fold_in(_gk, 2), (200000,), 0, 12500, jnp.int32)
        dst = jnp.minimum((12500 * jax.random.uniform(jax.random.fold_in(_gk, 3), (200000,)) ** 2.0).astype(jnp.int32), 99999)
        _o = jnp.argsort(dst, stable=True)
        src = src[_o]
        dst = dst[_o]
        edge_attr_32 = 0.000279952 + 1.00013 * jax.random.normal(jax.random.fold_in(_gk, 13), (200000, 32), jnp.float32)
        edge_type_4 = jax.random.randint(jax.random.fold_in(_gk, 15), (200000,), 0, 4, jnp.int32)
        edge_weight = jax.random.uniform(jax.random.fold_in(_gk, 16), (200000,), jnp.float32, 0.0, 1)
        return (x, src, dst, edge_attr_32, edge_type_4, edge_weight)
    x, src, dst, edge_attr_32, edge_type_4, edge_weight = _rec_inputs()

    def _L0_gnn_setup():
        import jax, jax.numpy as jnp
        import numpy as np
        N_NODES = 12500
        IN_FEATURES = 128
        OUT_FEATURES = 128
        N_EDGES = 400000
        key = jax.random.key(seed)
        k1, k2, k3, k4, k5 = jax.random.split(key, 5)
        node_features = jax.random.normal(k1, (N_NODES, IN_FEATURES), dtype=jnp.float32)
        edge_index = jax.random.randint(k2, (2, N_EDGES), 0, N_NODES, dtype=jnp.int64)
        edge_values = jax.random.uniform(k3, (N_EDGES,), dtype=jnp.float32)
        bound = 1.0 / np.sqrt(IN_FEATURES)
        W = jax.random.uniform(k4, (OUT_FEATURES, IN_FEATURES), minval=-bound, maxval=bound, dtype=jnp.float32)
        b = jax.random.uniform(k5, (OUT_FEATURES,), minval=-bound, maxval=bound, dtype=jnp.float32)
        return {'node_features': node_features, 'edge_index': edge_index, 'edge_values': edge_values, 'W': W, 'b': b}
    _L0_gnn_all = _L0_gnn_setup()
    _L0_gnn_in = {k: v for k, v in _L0_gnn_all.items() if k in ('W', 'b')}
    del _L0_gnn_all

    def _L1_gnn_setup():
        import jax, jax.numpy as jnp
        import numpy as np
        N_NODES = 25000
        N_EDGES = 80000
        D_NODE = 128
        D_EDGE = 32
        HIDDEN = 128
        key = jax.random.key(seed)
        ks = jax.random.split(key, 8)
        x = jax.random.normal(ks[0], (N_NODES, D_NODE), dtype=jnp.float32)
        edge_index = jax.random.randint(ks[1], (2, N_EDGES), 0, N_NODES, dtype=jnp.int64)
        edge_attr = jax.random.normal(ks[2], (N_EDGES, D_EDGE), dtype=jnp.float32)
        u = jax.random.normal(ks[3], (64, D_NODE), dtype=jnp.float32)
        batch = jax.random.randint(ks[4], (N_NODES,), 0, 64, dtype=jnp.int64)

        def xavier(k, fan_in, fan_out):
            limit = float(np.sqrt(6.0 / (fan_in + fan_out)))
            return jax.random.uniform(k, (fan_in, fan_out), jnp.float32, -limit, limit)
        W1 = xavier(ks[5], D_EDGE + D_NODE, HIDDEN)
        b1 = jnp.full((HIDDEN,), 0.01, dtype=jnp.float32)
        W2 = xavier(ks[6], HIDDEN + D_NODE, D_NODE)
        b2 = jnp.full((D_NODE,), 0.01, dtype=jnp.float32)
        return {'x': x, 'edge_index': edge_index, 'edge_attr': edge_attr, 'u': u, 'batch': batch, 'W1': W1, 'b1': b1, 'W2': W2, 'b2': b2}
    _L1_gnn_all = _L1_gnn_setup()
    _L1_gnn_in = {k: v for k, v in _L1_gnn_all.items() if k in ('u', 'W1', 'b1', 'W2', 'b2')}
    del _L1_gnn_all

    def _L2_gnn_setup():
        import jax, jax.numpy as jnp
        import numpy as np
        N = 12500
        E = 200000
        D_IN = 128
        D_HID = 128
        D_OUT = 128

        def _weighted_sage_conv(x, src, dst, edge_weight, deg, Wl, Wr):
            w = edge_weight / jnp.maximum(deg, 1e-12)[dst]
            msgs = w[:, None] * x[src]
            agg = jax.ops.segment_sum(msgs, dst, num_segments=x.shape[0])
            agg = agg / jnp.maximum(deg, 1.0)[:, None]
            return agg @ Wl.T + x @ Wr.T
        key = jax.random.key(seed)
        ks = jax.random.split(key, 7)
        x = jax.random.normal(ks[0], (N, D_IN), dtype=jnp.float32)
        edge_index = jax.random.randint(ks[1], (2, E), 0, N, dtype=jnp.int64)
        edge_weight = jax.random.uniform(ks[2], (E,), dtype=jnp.float32)
        s = 1.0 / np.sqrt(D_IN)
        W1l = jax.random.uniform(ks[3], (D_HID, D_IN), jnp.float32, -s, s)
        W1r = jax.random.uniform(ks[4], (D_HID, D_IN), jnp.float32, -s, s)
        s2 = 1.0 / np.sqrt(D_HID)
        W2l = jax.random.uniform(ks[5], (D_OUT, D_HID), jnp.float32, -s2, s2)
        W2r = jax.random.uniform(ks[6], (D_OUT, D_HID), jnp.float32, -s2, s2)
        return {'x': x, 'edge_index': edge_index, 'edge_weight': edge_weight, 'W1l': W1l, 'W1r': W1r, 'W2l': W2l, 'W2r': W2r}
    _L2_gnn_all = _L2_gnn_setup()
    _L2_gnn_in = {k: v for k, v in _L2_gnn_all.items() if k in ('W1l', 'W1r', 'W2l', 'W2r')}
    del _L2_gnn_all

    def _L3_gnn_setup():
        import jax, jax.numpy as jnp
        import numpy as np
        N = 12500
        E = 200000
        D = 128
        G = 128
        K = 4
        STEPS = 3

        def _gru_cell(a, h, W_ih, b_ih, W_hh, b_hh):
            gi = a @ W_ih.T + b_ih
            gh = h @ W_hh.T + b_hh
            ir, iz, in_ = jnp.split(gi, 3, axis=1)
            hr, hz, hn = jnp.split(gh, 3, axis=1)
            r = jax.nn.sigmoid(ir + hr)
            z = jax.nn.sigmoid(iz + hz)
            n = jnp.tanh(in_ + r * hn)
            return (1.0 - z) * n + z * h
        key = jax.random.key(seed)
        ks = jax.random.split(key, 16)
        s = 0.05
        return {'features': jax.random.normal(ks[0], (N, D), jnp.float32), 'src': jax.random.randint(ks[1], (E,), 0, N, jnp.int32), 'dst': jax.random.randint(ks[2], (E,), 0, N, jnp.int32), 'etypes': jax.random.randint(ks[3], (E,), 0, K, jnp.int32), 'W_et': jax.random.normal(ks[4], (K, D, D), jnp.float32) * s, 'b_et': jax.random.normal(ks[5], (K, D), jnp.float32) * s, 'W_ih': jax.random.normal(ks[6], (3 * D, D), jnp.float32) * s, 'b_ih': jax.random.normal(ks[7], (3 * D,), jnp.float32) * s, 'W_hh': jax.random.normal(ks[8], (3 * D, D), jnp.float32) * s, 'b_hh': jax.random.normal(ks[9], (3 * D,), jnp.float32) * s, 'i_w': jax.random.normal(ks[10], (G, D + D), jnp.float32) * s, 'i_b': jax.random.normal(ks[11], (G,), jnp.float32) * s, 'j_w': jax.random.normal(ks[12], (G, D), jnp.float32) * s, 'j_b': jax.random.normal(ks[13], (G,), jnp.float32) * s}
    _L3_gnn_all = _L3_gnn_setup()
    _L3_gnn_in = {k: v for k, v in _L3_gnn_all.items() if k in ('W_et', 'b_et', 'W_ih', 'b_ih', 'W_hh', 'b_hh', 'i_w', 'i_b', 'j_w', 'j_b')}
    del _L3_gnn_all
    return {'x': x, 'src': src, 'dst': dst, 'edge_attr_32': edge_attr_32, 'edge_type_4': edge_type_4, 'edge_weight': edge_weight, 'L0_gnn_W': _L0_gnn_in['W'], 'L0_gnn_b': _L0_gnn_in['b'], 'L1_gnn_u': _L1_gnn_in['u'], 'L1_gnn_W1': _L1_gnn_in['W1'], 'L1_gnn_b1': _L1_gnn_in['b1'], 'L1_gnn_W2': _L1_gnn_in['W2'], 'L1_gnn_b2': _L1_gnn_in['b2'], 'L2_gnn_W1l': _L2_gnn_in['W1l'], 'L2_gnn_W1r': _L2_gnn_in['W1r'], 'L2_gnn_W2l': _L2_gnn_in['W2l'], 'L2_gnn_W2r': _L2_gnn_in['W2r'], 'L3_gnn_W_et': _L3_gnn_in['W_et'], 'L3_gnn_b_et': _L3_gnn_in['b_et'], 'L3_gnn_W_ih': _L3_gnn_in['W_ih'], 'L3_gnn_b_ih': _L3_gnn_in['b_ih'], 'L3_gnn_W_hh': _L3_gnn_in['W_hh'], 'L3_gnn_b_hh': _L3_gnn_in['b_hh'], 'L3_gnn_i_w': _L3_gnn_in['i_w'], 'L3_gnn_i_b': _L3_gnn_in['i_b'], 'L3_gnn_j_w': _L3_gnn_in['j_w'], 'L3_gnn_j_b': _L3_gnn_in['j_b']}

def reference(x, src, dst, edge_attr_32, edge_type_4, edge_weight, L0_gnn_W, L0_gnn_b, L1_gnn_u, L1_gnn_W1, L1_gnn_b1, L1_gnn_W2, L1_gnn_b2, L2_gnn_W1l, L2_gnn_W1r, L2_gnn_W2l, L2_gnn_W2r, L3_gnn_W_et, L3_gnn_b_et, L3_gnn_W_ih, L3_gnn_b_ih, L3_gnn_W_hh, L3_gnn_b_hh, L3_gnn_i_w, L3_gnn_i_b, L3_gnn_j_w, L3_gnn_j_b):
    import jax
    import jax.numpy as jnp

    def _L0_gnn_ref(node_features, edge_index, edge_values, W, b):
        import jax, jax.numpy as jnp
        import numpy as np
        N_NODES = 12500
        IN_FEATURES = 128
        OUT_FEATURES = 128
        N_EDGES = 400000
        n_nodes = node_features.shape[0]
        row, col = (edge_index[0], edge_index[1])
        vals = jnp.where(row != col, edge_values, jnp.zeros_like(edge_values)) ** 2
        wx = node_features @ W.T + b
        messages = vals[:, None] * wx[col]
        temp = jax.ops.segment_sum(messages, row, num_segments=n_nodes)
        return wx * temp

    def _L1_gnn_ref(x, edge_index, edge_attr, u, batch, W1, b1, W2, b2):
        import jax, jax.numpy as jnp
        import numpy as np
        N_NODES = 25000
        N_EDGES = 80000
        D_NODE = 128
        D_EDGE = 32
        HIDDEN = 128
        row, col = (edge_index[0], edge_index[1])
        msg = jnp.concatenate([x[row], edge_attr], axis=1)
        msg = msg @ W1 + b1
        agg = jax.ops.segment_sum(msg, col, num_segments=x.shape[0])
        out = jnp.concatenate([x, agg], axis=1)
        return out @ W2 + b2

    def _L2_gnn_ref(x, edge_index, edge_weight, W1l, W1r, W2l, W2r):
        import jax, jax.numpy as jnp
        import numpy as np
        N = 12500
        E = 200000
        D_IN = 128
        D_HID = 128
        D_OUT = 128

        def _weighted_sage_conv(x, src, dst, edge_weight, deg, Wl, Wr):
            w = edge_weight / jnp.maximum(deg, 1e-12)[dst]
            msgs = w[:, None] * x[src]
            agg = jax.ops.segment_sum(msgs, dst, num_segments=x.shape[0])
            agg = agg / jnp.maximum(deg, 1.0)[:, None]
            return agg @ Wl.T + x @ Wr.T
        src, dst = (edge_index[0], edge_index[1])
        deg = jax.ops.segment_sum(jnp.ones_like(edge_weight), dst, num_segments=x.shape[0])
        h = _weighted_sage_conv(x, src, dst, edge_weight, deg, W1l, W1r)
        h = jax.nn.relu(h)
        out = _weighted_sage_conv(h, src, dst, edge_weight, deg, W2l, W2r)
        return out

    def _L3_gnn_ref(features, src, dst, etypes, W_et, b_et, W_ih, b_ih, W_hh, b_hh, i_w, i_b, j_w, j_b):
        import jax, jax.numpy as jnp
        import numpy as np
        N = 12500
        E = 200000
        D = 128
        G = 128
        K = 4
        STEPS = 3

        def _gru_cell(a, h, W_ih, b_ih, W_hh, b_hh):
            gi = a @ W_ih.T + b_ih
            gh = h @ W_hh.T + b_hh
            ir, iz, in_ = jnp.split(gi, 3, axis=1)
            hr, hz, hn = jnp.split(gh, 3, axis=1)
            r = jax.nn.sigmoid(ir + hr)
            z = jax.nn.sigmoid(iz + hz)
            n = jnp.tanh(in_ + r * hn)
            return (1.0 - z) * n + z * h
        n_nodes = features.shape[0]
        h = features
        for _ in range(STEPS):
            t = jnp.einsum('nd,kod->kno', h, W_et) + b_et[:, None, :]
            msg = t[etypes, src]
            a = jax.ops.segment_sum(msg, dst, num_segments=n_nodes)
            h = _gru_cell(a, h, W_ih, b_ih, W_hh, b_hh)
        gate = jax.nn.sigmoid(jnp.concatenate([h, features], axis=1) @ i_w.T + i_b)
        return gate * (h @ j_w.T + j_b)
    edge_index = jnp.stack([src, dst])
    batch0 = jnp.zeros((12500,), jnp.int32)
    x = _layernorm(x + _L0_gnn_ref(x, edge_index, edge_weight, L0_gnn_W, L0_gnn_b), axis=-1)
    x = _layernorm(x + _L1_gnn_ref(x, edge_index, edge_attr_32, L1_gnn_u, batch0, L1_gnn_W1, L1_gnn_b1, L1_gnn_W2, L1_gnn_b2), axis=-1)
    x = _layernorm(x + _L2_gnn_ref(x, edge_index, edge_weight, L2_gnn_W1l, L2_gnn_W1r, L2_gnn_W2l, L2_gnn_W2r), axis=-1)
    x = _layernorm(x + _L3_gnn_ref(x, src, dst, edge_type_4, L3_gnn_W_et, L3_gnn_b_et, L3_gnn_W_ih, L3_gnn_b_ih, L3_gnn_W_hh, L3_gnn_b_hh, L3_gnn_i_w, L3_gnn_i_b, L3_gnn_j_w, L3_gnn_j_b), axis=-1)
    return x

_drawn_inputs = setup_inputs


def setup_inputs(seed=0):
    import zlib

    import numpy as np

    out = dict(_drawn_inputs(seed))
    spreads = {'L1_gnn_b1': (0.009999999776482582, 0.6), 'L1_gnn_b2': (0.009999999776482582, 0.6)}
    factors = {'L2_gnn_W1l': 8.0,
     'L2_gnn_W2l': 6.337,
     'L3_gnn_b_ih': 3.959,
     'L3_gnn_b_hh': 6.562,
     'L3_gnn_i_b': 8.0}
    for name, (base, spread) in spreads.items():
        noise = np.random.default_rng([zlib.crc32(name.encode()), seed]).standard_normal(out[name].shape)
        drawn = base * np.exp(spread * noise) if base else spread * noise
        out[name] = jnp.asarray(drawn.astype(out[name].dtype))
    for name, factor in factors.items():
        out[name] = (out[name] * factor).astype(out[name].dtype)
    return out
```

```python
from contextlib import ExitStack

import concourse.bass as bass
from concourse import mybir

F32 = mybir.dt.float32
I32 = mybir.dt.int32
U32 = mybir.dt.uint32
U16 = mybir.dt.uint16
ALU = mybir.AluOpType
ACT = mybir.ActivationFunctionType

P = 128
D = 128
DE = 32
KT = 4
N = 12500
E = 200000
A = 4
GN = A * P
NG = -(-N // GN)
NT = NG * A
NPAD = NG * GN
LASTP = (N - (NG - 1) * GN) // A
U = 16
NQ = 4
EC = U * -(-E // (P * U))
ETAIL = E - (P - 1) * EC
STURNS = EC // U
FULLTURNS = ETAIL // U
NCH = U * -(-((E + (P - 1) * NT) // P) // U)
TURNS = NCH // U
IPC = NCH // P
RS = 3
RD = DE + 5
BLK = 26
NBLK = NCH // BLK
ZD, ZS = NCH // 32, NCH // 8
EPS = 1e-5
FAR = float(2 ** 20)
NW = 20
W_0, W_1L, W_1R, W_2L, W_2R, W_ET, W_IH, W_HH, W_I, W_J, W_1A, W_1B = 0, 1, 2, 3, 4, 5, 9, 12, 15, 17, 18, 19
WEIGHT_DMAS = NW + 1 + 3 + A + KT + 4
assert ETAIL % U == 0 and NCH % P == 0 and NCH % BLK == 0 and NG % 2 == 1 and (N - (NG - 1) * GN) % A == 0
assert ((P - 1) * NCH + ((int(FAR) - 1) >> 7)) >= P * NCH


def build(nc, x, src, dst, edge_attr_32, edge_type_4, edge_weight, L0_gnn_W, L0_gnn_b, L1_gnn_u, L1_gnn_W1,
          L1_gnn_b1, L1_gnn_W2, L1_gnn_b2, L2_gnn_W1l, L2_gnn_W1r, L2_gnn_W2l, L2_gnn_W2r, L3_gnn_W_et,
          L3_gnn_b_et, L3_gnn_W_ih, L3_gnn_b_ih, L3_gnn_W_hh, L3_gnn_b_hh, L3_gnn_i_w, L3_gnn_i_b, L3_gnn_j_w,
          L3_gnn_j_b, out):
    ctx = ExitStack()
    with ctx:
        def sb(name, shape, dt=F32):
            return ctx.enter_context(nc.sbuf_tensor(name, shape, dt))

        def sem(name):
            return ctx.enter_context(nc.semaphore(name))

        def dram(name, shape, dt=F32):
            return nc.dram_tensor(name, shape, dt, kind="Internal").ap()

        X0 = dram("t_x0", [NPAD, D])
        WX = dram("t_wx", [NPAD, D])
        X1 = dram("t_x1", [NPAD, D])
        X2 = dram("t_x2", [NPAD, D])
        H1 = dram("t_h1", [NPAD, D])
        X3 = dram("t_x3", [NPAD, D])
        TT = dram("t_types", [NPAD, KT * D])
        SRC_REC = dram("src_records", [P * NCH, RS])
        DST_REC = dram("dst_records", [P * NCH, RD])
        SRC_OFF = dram("src_tile_offsets", [NCH], I32)
        DST_OFF = dram("dst_tile_offsets", [NCH], I32)

        acc = sb("acc", [P, NT * P])
        aux = sb("aux", [P, NT * P])
        meta_low = sb("meta_low", [P, NCH])
        meta_w = sb("meta_w", [P, NCH])
        meta_src = sb("meta_src", [P, NCH], U16)
        meta_row = sb("meta_row", [P, NCH], U16)
        tile_off = sb("tile_off", [1, NCH], I32)
        ring = sb("ring", [P, 2 * U, P])
        msg, hot = ring[:, 0:U, :], ring[:, U:2 * U, :]
        stage = sb("stage", [P, U], U32)
        rec = sb("rec", [P, U, RD])
        srec = sb("srec", [P, U, RS])
        wT = sb("wT", [P, NW, P])
        w2a = sb("w2a", [P, D])
        w2b = sb("w2b", [P, D])
        c1 = sb("c1", [P, D])
        c2 = sb("c2", [DE + 1, D])
        b0_row = sb("b0_row", [1, D])
        b2_all = sb("b2_all", [P, GN])
        bet_all = sb("bet_all", [P, KT * D])
        gru_b = sb("gru_b", [P, 6])
        gru_rz = sb("gru_rz", [P, 2])
        ib_col = sb("ib_col", [P, 1])
        jb_col = sb("jb_col", [P, 1])
        eps_col = sb("eps_col", [P, 1])
        ones_f = sb("ones_f", [P, P])
        ident = sb("ident", [P, P])
        before = sb("before", [P, P])
        iota_i = sb("iota_i", [P, P], I32)
        iota_f = sb("iota_f", [P, P])
        chunk_i = sb("chunk_i", [P, IPC], I32)
        chunk_f = sb("chunk_f", [P, IPC])
        deg_pick = sb("deg_pick", [DE + 1, 1])
        hist = sb("hist", [P, NT])
        base = sb("base", [P, NT])
        cnt_i = sb("cnt_i", [P, NT], I32)
        cnt_f = sb("cnt_f", [P, NT])
        cum = sb("cum", [P, NT])
        spare = sb("spare", [P, NT])
        tid = sb("tid", [P, IPC])
        tid_i = sb("tid_i", [P, IPC], I32)
        rdeg = sb("rdeg", [P, NT])
        xin = sb("xin", [P, 2, GN])
        yin = sb("yin", [P, 2, GN])
        xT = sb("xT", [P, 2, GN])
        accs = sb("accs", [P, 2, GN])
        auxs = sb("auxs", [P, 2, GN])
        z = sb("z", [P, GN])
        y = sb("y", [P, GN])
        res = sb("res", [P, 2, GN])
        wide = sb("wide", [P, 2, 2 * KT * D])
        stats = sb("stats", [P, A, 6])
        mv = sb("mv", [P, A, 2])
        std = sb("std", [P, A])
        rstd = sb("rstd", [P, A])

        def part(t, k, n=1, dt=None):
            v = t[:, k * EC:(k + n) * EC]
            return v if dt is None else v.bitcast(dt)
        s_key, s_tile, s_mask, s_scan, s_pos = (part(acc, k) for k in range(5))
        s_rec = part(acc, 5, RS).rearrange("p (e w) -> p e w", w=RS)
        d_key, d_tile, d_pos = (part(aux, k) for k in range(3))
        d_rec = part(aux, 3, 5).rearrange("p (e w) -> p e w", w=5)
        srcmeta = aux[:, 0:RS * NCH].rearrange("p (c w) -> p c w", w=RS)
        field = wide[:, :, 0:BLK * RD]
        zero_rec = wide[:, :, :].rearrange("p a b -> p (a b)")[:, 0:ZD * RD]
        zero_src = yin[:, :, :].rearrange("p a b -> p (a b)")[:, 0:ZS * RS]

        bank = [ctx.enter_context(nc.psum_tensor(f"bank{i}", [P, 512], F32)) for i in range(8)]

        tails_set = sem("tails_set")
        zeros_set = sem("zeros_set")
        x0_out = sem("x0_out")
        feat_added = sem("feat_added")
        const_ready = sem("const_ready")
        pool_const = sem("pool_const")
        weights_in = sem("weights_in")
        weights_turned = sem("weights_turned")
        weights_ready = sem("weights_ready")
        keys_in = sem("keys_in")
        zeros_out = sem("zeros_out")
        chain = sem("chain")
        hist_ready = sem("hist_ready")
        base_sums = sem("base_sums")
        pos_ready = sem("pos_ready")
        off_ready = sem("off_ready")
        off_out = sem("off_out")
        off_in = sem("off_in")
        srcmeta_in = sem("srcmeta_in")
        staged = [sem(f"staged{q}") for q in range(NQ)]
        attr_in = [sem(f"attr_in{q}") for q in range(NQ)]
        slot_dma = [sem(f"slot_dma{u}") for u in range(U)]
        block_in = [sem(f"block_in{i}") for i in range(2)]
        block_read = sem("block_read")
        hot_ready = [sem(f"hot_ready{q}") for q in range(NQ)]
        summed = [sem(f"summed{q}") for q in range(NQ)]
        added = sem("added")
        pool_seen = sem("pool_seen")
        vec_seen = sem("vec_seen")

        class Dense:
            def __init__(self, name):
                self.ld = [sem(f"{name}_in{i}") for i in range(2)]
                self.turned = sem(f"{name}_turned")
                self.copied = sem(f"{name}_copied")
                self.prod = sem(f"{name}_prod")
                self.free = sem(f"{name}_free")
                self.var = sem(f"{name}_var")
                self.std = sem(f"{name}_std")
                self.rows = sem(f"{name}_rows")
                self.st = [sem(f"{name}_out{i}") for i in range(2)]

        p_wx, p_l0, p_l1, p_l2a, p_l2b, p_t, p_fin = (Dense(n) for n in ("wx", "l0", "l1", "l2a", "l2b", "tt", "fin"))
        gate_prod = sem("gate_prod")
        gate_rz = sem("gate_rz")
        gate_pre = sem("gate_pre")
        gate_n = sem("gate_n")
        h_ready = sem("h_ready")
        h_copied = sem("h_copied")
        t_prod = [sem(f"t_prod{i}") for i in range(2)]
        t_rows = [sem(f"t_rows{i}") for i in range(2)]
        t_out = [sem(f"t_out{i}") for i in range(2)]


        def rows(t, g):
            v = t[g * GN:(g + 1) * GN, :] if isinstance(g, int) else t[bass.ds(g * GN, GN), :]
            return v.rearrange("(p a) f -> p (a f)", a=A)

        def groups(eng, step):
            with eng.Fori(0, NG // 2) as j:
                step(j, 0)
                step(j, 1)
            step(NG // 2, 0)

        def cols(t, start, n):
            return t[:, start:start + n] if isinstance(start, int) else t[:, bass.ds(start, n)]

        block = ctx.enter_context(nc.Block())

        @block.sync
        def _(sp):
            def edges_in(tile, a):
                v = a[0:(P - 1) * EC].rearrange("(p e) -> p e", e=EC)
                for lo, hi in ((0, 112), (112, P - 1)):
                    sp.dma_start(tile[lo:hi, :], v[lo:hi, :]).then_inc(keys_in, 16)
                sp.dma_start(tile[P - 1:P, 0:ETAIL], a[(P - 1) * EC:E].rearrange("(p e) -> p e", p=1)).then_inc(keys_in, 16)

            sp.wait_ge(tails_set, 4)
            edges_in(s_key.bitcast(I32), src)
            edges_in(d_key.bitcast(I32), dst)
            edges_in(meta_w[:, 0:EC], edge_weight)
            edges_in(meta_low[:, 0:EC].bitcast(I32), edge_type_4)

            w_in = [L0_gnn_W, L2_gnn_W1l, L2_gnn_W1r, L2_gnn_W2l, L2_gnn_W2r]
            w_in += [L3_gnn_W_et[k] for k in range(KT)]
            w_in += [w[c * D:(c + 1) * D, :] for w in (L3_gnn_W_ih, L3_gnn_W_hh) for c in range(3)]
            w_in += [L3_gnn_i_w[:, 0:D], L3_gnn_i_w[:, D:2 * D], L3_gnn_j_w, L1_gnn_W1[0:D, :]]
            for i, w in enumerate(w_in):
                sp.dma_start(ring[:, i, :], w).then_inc(weights_in, 16)
            sp.dma_start(ring[0:DE, NW - 1, :], L1_gnn_W1[D:D + DE, :]).then_inc(weights_in, 16)
            sp.dma_start(ring[DE:DE + 1, NW - 1, :], L1_gnn_b1.rearrange("(a d) -> a d", a=1)).then_inc(weights_in, 16)
            sp.dma_start(w2a[:, :], L1_gnn_W2[0:D, :]).then_inc(weights_in, 16)
            sp.dma_start(w2b[:, :], L1_gnn_W2[D:2 * D, :]).then_inc(weights_in, 16)
            sp.dma_start(b0_row[:, :], L0_gnn_b.rearrange("(a d) -> a d", a=1)).then_inc(weights_in, 16)
            for a in range(A):
                sp.dma_start(b2_all[:, a * D:(a + 1) * D],
                             L1_gnn_b2.rearrange("(a d) -> a d", a=1).to_broadcast([P, D])).then_inc(weights_in, 16)
            for k in range(KT):
                sp.dma_start(bet_all[:, k * D:(k + 1) * D],
                             L3_gnn_b_et[k:k + 1, :].to_broadcast([P, D])).then_inc(weights_in, 16)
            with nc.allow_non_contiguous_dma(reason="bias columns, a few hundred elements"):
                sp.dma_start(gru_b[:, 0:3], L3_gnn_b_ih.rearrange("(c p) -> p c", p=P)).then_inc(weights_in, 16)
                sp.dma_start(gru_b[:, 3:6], L3_gnn_b_hh.rearrange("(c p) -> p c", p=P)).then_inc(weights_in, 16)
                sp.dma_start(ib_col[:, :], L3_gnn_i_b.rearrange("(p a) -> p a", a=1)).then_inc(weights_in, 16)
                sp.dma_start(jb_col[:, :], L3_gnn_j_b.rearrange("(p a) -> p a", a=1)).then_inc(weights_in, 16)

            sp.dma_start(X0[0:N, :], x).then_inc(x0_out, 16)
            sp.wait_ge(zeros_set, 1)
            sp.dma_start(rows(X0, NG - 1)[LASTP:P, :], z[LASTP:P, :]).then_inc(x0_out, 16)
            src_empty = SRC_REC.rearrange("(l c) w -> l (c w)", c=NCH)
            for i in range(NCH // ZS):
                sp.dma_start(src_empty[:, i * ZS * RS:(i + 1) * ZS * RS], zero_src).then_inc(zeros_out, 16)
            dst_empty = DST_REC.rearrange("(l c) w -> l (c w)", c=NCH)
            for i in range(NCH // ZD):
                sp.dma_start(dst_empty[:, i * ZD * RD:(i + 1) * ZD * RD], zero_rec).then_inc(zeros_out, 16)

            def pass_rows(d, loads, store):
                for slot, t in loads:
                    sp.dma_start(slot[:, 0, :], rows(t, 0)).then_inc(d.ld[0], 16)

                def step(j, par):
                    g = 2 * j + par
                    if not (isinstance(g, int) and g == NG - 1):
                        if isinstance(g, int) is False or g > 0:
                            sp.wait_ge(d.rows, g)
                        for slot, t in loads:
                            sp.dma_start(slot[:, 1 - par, :], rows(t, g + 1)).then_inc(d.ld[1 - par], 16)
                    sp.wait_ge(d.rows, g + 1)
                    store(g, par)
                groups(sp, step)
                for par in range(2):
                    sp.wait_ge(d.st[par], 16 * (NG // 2 + 1 - par))

            def to_table(d, t):
                def store(g, par):
                    sp.dma_start(rows(t, g), res[:, par, :]).then_inc(d.st[par], 16)
                return store

            sp.wait_ge(x0_out, 32)
            pass_rows(p_wx, [(xin, X0)], to_table(p_wx, WX))

            for n, t in ((1, SRC_OFF), (2, DST_OFF)):
                sp.wait_ge(off_ready, n)
                sp.dma_start(t.rearrange("(p c) -> p c", p=P), tid_i[:, :]).then_inc(off_out, 16)

            attr = edge_attr_32[0:(P - 1) * EC, :].rearrange("(p e) f -> p e f", e=EC)
            attr_tail = edge_attr_32[(P - 1) * EC:E, :].rearrange("(p e) f -> p e f", p=1)

            def attr_turn(t, whole):
                for q in range(NQ):
                    for u in range(q * 4, q * 4 + 4):
                        sp.wait_ge(slot_dma[u], (t + STURNS) * 16)
                    c = t * U + q * 4
                    for lo, hi in ((0, 112), (112, P - 1)):
                        sp.dma_start(rec[lo:hi, q * 4:q * 4 + 4, 0:DE],
                                     attr[lo:hi, bass.ds(c, 4), :]).then_inc(attr_in[q], 16)
                    if whole:
                        sp.dma_start(rec[P - 1:P, q * 4:q * 4 + 4, 0:DE],
                                     attr_tail[:, bass.ds(c, 4), :]).then_inc(attr_in[q], 16)
            with sp.Fori(0, FULLTURNS) as t:
                attr_turn(t, True)
            with sp.Fori(FULLTURNS, STURNS) as t:
                attr_turn(t, False)

            for u in range(U):
                sp.wait_ge(slot_dma[u], 16 * 2 * STURNS)
            sp.dma_start(aux[:, 0:RS * NCH], src_empty).then_inc(srcmeta_in, 16)
            sp.wait_ge(off_out, 32)
            sp.dma_start(tile_off[:, :], SRC_OFF.rearrange("(a c) -> a c", a=1)).then_inc(off_in, 16)

            with sp.Fori(0, NBLK // 2) as j:
                sp.wait_ge(block_read, 2 * j)
                for par in range(2):
                    sp.dma_start(field[:, par, :], dst_empty[:, bass.ds((2 * j + par) * BLK * RD, BLK * RD)]
                                 ).then_inc(block_in[par], 16)

            pass_rows(p_l0, [(xin, X0), (yin, WX)], to_table(p_l0, X1))

            sp.wait_ge(added, NCH)
            sp.dma_start(tile_off[:, :], DST_OFF.rearrange("(a c) -> a c", a=1)).then_inc(off_in, 16)
            with sp.Fori(0, TURNS) as t:
                for q in range(NQ):
                    sp.wait_ge(summed[q], t + TURNS)
                    sp.dma_start(rec[:, q * 4:q * 4 + 4, :].rearrange("p c w -> p (c w)"),
                                 dst_empty[:, bass.ds((t * U + q * 4) * RD, 4 * RD)]).then_inc(attr_in[q], 16)

            pass_rows(p_l1, [(xin, X1)], to_table(p_l1, X2))
            pass_rows(p_l2a, [(xin, X2)], to_table(p_l2a, H1))
            pass_rows(p_l2b, [(xin, H1), (yin, X2)], to_table(p_l2b, X3))

            def t_store(n, g):
                half = A // 2 * KT * D
                for hh in range(2):
                    sp.wait_ge(t_rows[hh], n * NG + g + 1)
                    row = TT[bass.ds(g * GN, GN), :].rearrange("(p a) f -> p (a f)", a=A)
                    sp.dma_start(row[:, hh * half:(hh + 1) * half], wide[:, hh, :]).then_inc(t_out[hh], 16)

            sp.dma_start(xin[:, 0, :], rows(X3, 0)).then_inc(p_t.ld[0], 16)

            def t_step(j, par):
                g = 2 * j + par
                if not (isinstance(g, int) and g == NG - 1):
                    if not isinstance(g, int) or g > 0:
                        sp.wait_ge(p_t.turned, g)
                    sp.dma_start(xin[:, 1 - par, :], rows(X3, g + 1)).then_inc(p_t.ld[1 - par], 16)
                t_store(0, g)
            groups(sp, t_step)
            for n in (1, 2):
                with sp.Fori(0, NG) as g:
                    t_store(n, g)

            def to_out(g, par):
                if isinstance(g, int) and g == NG - 1:
                    sp.dma_start(out[g * GN:N, :].rearrange("(p a) f -> p (a f)", a=A),
                                 res[0:LASTP, par, :]).then_inc(p_fin.st[par], 16)
                else:
                    sp.dma_start(rows(out, g), res[:, par, :]).then_inc(p_fin.st[par], 16)
            pass_rows(p_fin, [(xin, X3)], to_out)

        @block.gpsimd
        def _(pool):
            pool.memset(ones_f[:, :], 1.0)
            pool.memset(eps_col[:, :], EPS)
            pool.iota(iota_i[:, :], pattern=[[1, P]], base=0, channel_multiplier=0)
            pool.iota(chunk_i[:, :], pattern=[[1, IPC]], base=0, channel_multiplier=IPC).then_inc(pool_const, 1)
            pool.wait_ge(pool_const, 1)
            pool.affine_select(out=ident[:, :], in_=ones_f[:, :], compare_op=ALU.is_equal, fill=0.0, base=0,
                               pattern=[[-1, P]], channel_multiplier=1)
            pool.affine_select(out=before[:, :], in_=ones_f[:, :], compare_op=ALU.is_gt, fill=0.0, base=0,
                               pattern=[[1, P]], channel_multiplier=-1)
            pool.affine_select(out=deg_pick[:, :], in_=ones_f[0:DE + 1, 0:1], compare_op=ALU.is_equal, fill=0.0,
                               base=-DE, pattern=[[0, 1]], channel_multiplier=1).then_inc(const_ready, 1)
            pool.memset(z[:, :], 0.0)
            pool.memset(zero_src, 0.0)
            pool.memset(zero_rec, 0.0).then_inc(pool_const, 1)
            pool.wait_ge(pool_const, 2)
            pool.memset(zero_src.rearrange("p (c w) -> p c w", w=RS)[:, :, 1:2], -1.0)
            pool.memset(zero_rec.rearrange("p (c w) -> p c w", w=RD)[:, :, DE + 1:DE + 2], -1.0).then_inc(zeros_set, 1)

            def go(q, n):
                pool.wait_ge(staged[q], n)
                pool.sem_inc(pool_seen, 1)

            pool.wait_ge(zeros_out, 16 * (NCH // ZS + NCH // ZD))
            pool.sem_inc(pool_seen, 1)

            def scatter(table, slot, n):
                def turn(t, whole=None):
                    for q in range(NQ):
                        go(q, n * STURNS + t + 1)
                        if whole is not None:
                            before_ = t * 48 if whole else t * 32 + 16 * FULLTURNS
                            pool.wait_ge(attr_in[q], before_ + (48 if whole else 32))
                            pool.sem_inc(pool_seen, 1)
                        for u in range(q * 4, q * 4 + 4):
                            pool.indirect_dma_start(
                                table, bass.IndirectOffsetOnAxis(ap=stage[:, u:u + 1], axis=0), slot[:, u, :], None,
                                bounds_check=P * NCH - 1, oob_is_err=False).then_inc(slot_dma[u], 16)
                return turn
            by_src = scatter(SRC_REC, srec, 0)
            with pool.Fori(0, STURNS) as t:
                by_src(t)
            by_dst = scatter(DST_REC, rec, 1)
            with pool.Fori(0, FULLTURNS) as t:
                by_dst(t, True)
            with pool.Fori(FULLTURNS, STURNS) as t:
                by_dst(t, False)

            def gather(ph, table):
                with pool.Fori(0, TURNS) as t:
                    for q in range(NQ):
                        go(q, 2 * STURNS + ph * TURNS + t + 1)
                        for u in range(q * 4, q * 4 + 4):
                            pool.indirect_dma_start(
                                msg[:, u, :], None, table, bass.IndirectOffsetOnAxis(ap=stage[:, u:u + 1], axis=0)
                            ).then_inc(slot_dma[u], 16)

            def table_out(d):
                for par in range(2):
                    pool.wait_ge(d.st[par], 16 * (NG // 2 + 1 - par))
                    pool.sem_inc(pool_seen, 1)

            for ph, (d, table) in enumerate(((p_wx, WX), (p_l0, X1), (p_l1, X2), (p_l2a, H1))):
                table_out(d)
                gather(ph, table)
            types = TT.rearrange("n (k f) -> (n k) f", k=KT)
            for n in range(3):
                for hh in range(2):
                    pool.wait_ge(t_out[hh], 16 * NG * (n + 1))
                    pool.sem_inc(pool_seen, 1)
                gather(4 + n, types)

        @block.scalar
        def _(act):
            for b in range(NW // 4):
                act.wait_ge(weights_turned, b + 1)
                n = 4 * P if b < NW // 4 - 1 else 3 * P + DE + 1
                act.activation(wT[:, 4 * b:4 * b + 4, :].rearrange("p a b -> p (a b)")[:, 0:n], bank[b][:, 0:n],
                               ACT.Copy).then_inc(weights_ready, 1)
            act.wait_ge(weights_turned, NW // 4 + 1)
            act.activation(c1[:, :], bank[5][:, 0:D], ACT.Copy)
            act.activation(c2[:, :], bank[5][0:DE + 1, D:2 * D], ACT.Copy).then_inc(weights_ready, 1)
            act.activation(gru_rz[:, 0:1], gru_b[:, 0:1], ACT.Identity, bias=gru_b[:, 3:4])
            act.activation(gru_rz[:, 1:2], gru_b[:, 1:2], ACT.Identity, bias=gru_b[:, 4:5]).then_inc(weights_ready, 1)

            def wx_step(j, par):
                g = 2 * j + par
                act.wait_ge(p_wx.turned, g + 1)
                act.activation(xT[:, par, :], bank[par][:, :], ACT.Copy).then_inc(p_wx.copied, 1)
                act.wait_ge(p_wx.prod, g + 1)
                act.wait_ge(p_wx.st[par], 16 * j)
                act.activation(res[:, par, :], bank[2 + par][:, :], ACT.Copy).then_inc(p_wx.rows, 1)
            groups(act, wx_step)

            def stage_records(n, pos, fields, slot):
                act.wait_ge(pos_ready, n + 1)
                with act.Fori(0, STURNS) as t:
                    for q in range(NQ):
                        for u in range(q * 4, q * 4 + 4):
                            act.wait_ge(slot_dma[u], (t + n * STURNS) * 16)
                        c = t * U + q * 4
                        act.activation(stage[:, q * 4:q * 4 + 4], cols(pos, c, 4), ACT.Copy)
                        act.activation(slot[:, q * 4:q * 4 + 4, :], fields[:, bass.ds(c, 4), :],
                                       ACT.Copy).then_inc(staged[q], 1)
            stage_records(0, s_pos, s_rec, srec)
            stage_records(1, d_pos, d_rec, rec[:, :, DE:RD])

            with act.Fori(0, NBLK // 2) as j:
                for par in range(2):
                    act.wait_ge(block_in[par], (j + 1) * 16)
                    f = field[:, par, :].rearrange("p (c w) -> p c w", w=RD)
                    for k, t in ((1, meta_low), (2, meta_w), (3, meta_src), (4, meta_row)):
                        ins = act.activation(cols(t, (2 * j + par) * BLK, BLK), f[:, :, DE + k], ACT.Copy)
                    ins.then_inc(block_read, 1)

            def sqrt_step(d):
                def step(j, par):
                    act.wait_ge(d.var, 2 * j + par + 1)
                    act.activation(std[:, :], mv[:, :, 1], ACT.Sqrt, bias=eps_col[:, 0:1]).then_inc(d.std, 1)
                return step

            def copy_step(d, features=False):
                def step(j, par):
                    g = 2 * j + par
                    act.wait_ge(d.prod, g)
                    act.activation(accs[:, par, :], cols(acc, g * GN, GN), ACT.Copy)
                    if features:
                        act.activation(auxs[0:DE + 1, par, :], cols(aux[0:DE + 1, :], g * GN, GN), ACT.Copy)
                    act.wait_ge(d.turned, g + 1)
                    act.activation(xT[:, par, :], bank[par][:, :], ACT.Copy).then_inc(d.copied, 1)
                return step

            def both(*steps):
                def step(j, par):
                    for s in steps:
                        s(j, par)
                return step

            groups(act, sqrt_step(p_l0))
            def sums_done(ph):
                act.wait_ge(added, (ph + 1) * NCH)

            sums_done(1)
            act.wait_ge(feat_added, NCH)
            groups(act, both(copy_step(p_l1, features=True), sqrt_step(p_l1)))
            sums_done(2)
            groups(act, copy_step(p_l2a))
            sums_done(3)
            groups(act, both(copy_step(p_l2b), sqrt_step(p_l2b)))

            def state_step(j, par):
                g = 2 * j + par
                act.wait_ge(p_t.turned, g + 1)
                act.activation(cols(aux, g * GN, GN), bank[par][:, :], ACT.Copy)
                act.wait_ge(t_prod[1], g)
                act.activation(auxs[:, 0, :], bank[par][:, :], ACT.Copy).then_inc(p_t.copied, 1)
            groups(act, state_step)

            for n in range(3):
                with act.Fori(0, NG) as g:
                    act.wait_ge(gate_prod, n * NG + g + 1)
                    act.activation(xT[:, 0, :], bank[0][:, :], ACT.Sigmoid, bias=gru_rz[:, 0:1])
                    act.activation(xT[:, 1, :], bank[1][:, :], ACT.Sigmoid, bias=gru_rz[:, 1:2]).then_inc(gate_rz, 1)
                    act.wait_ge(gate_pre, n * NG + g + 1)
                    act.activation(yin[:, 0, :], y[:, :], ACT.Tanh, bias=gru_b[:, 2:3]).then_inc(gate_n, 1)
                    if n < 2:
                        act.wait_ge(h_ready, n * NG + g + 1)
                        act.wait_ge(t_prod[1], (n + 1) * NG + g)
                        act.activation(auxs[:, 0, :], cols(aux, g * GN, GN), ACT.Copy).then_inc(h_copied, 1)

            def fin_step(j, par):
                g = 2 * j + par
                act.wait_ge(p_fin.turned, g + 1)
                act.activation(xT[:, par, :], bank[par][:, :], ACT.Copy).then_inc(p_fin.copied, 1)
                act.wait_ge(p_fin.prod, g + 1)
                act.activation(yin[:, par, :], bank[2][:, :], ACT.Sigmoid, bias=ib_col[:, 0:1]).then_inc(gate_rz, 1)
            groups(act, both(fin_step, sqrt_step(p_fin)))

        @block.tensor
        def _(pe):
            pe.wait_ge(const_ready, 1)
            pe.wait_ge(weights_in, 16 * WEIGHT_DMAS)
            for i in range(NW):
                rows_ = P if i < NW - 1 else DE + 1
                mm = pe.transpose(bank[i // 4][:, (i % 4) * P:(i % 4) * P + rows_], ring[0:rows_, i, :],
                                  ident[0:rows_, 0:rows_])
                if i % 4 == 3:
                    mm.then_inc(weights_turned, 1)
            pe.wait_ge(weights_ready, NW // 4)
            pe.matmul(bank[5][:, 0:D], wT[:, W_1A, :], w2b[:, :], start=True, stop=True)
            pe.matmul(bank[5][0:DE + 1, D:2 * D], wT[:, W_1B, 0:DE + 1], w2b[:, :], start=True,
                      stop=True).then_inc(weights_turned, 1)

            def sort_sums(n):
                pe.wait_ge(hist_ready, n + 1)
                pe.matmul(bank[6][:, 0:NT], before[:, :], hist[:, :], start=True, stop=True)
                pe.matmul(bank[6][:, P:P + NT], ones_f[:, :], hist[:, :], start=True, stop=True).then_inc(base_sums, 1)
            sort_sums(0)

            def turn_rows(d, j, par, loads=1):
                pe.wait_ge(d.ld[par], (j + 1) * 16 * loads)
                for a in range(A):
                    mm = pe.transpose(bank[par][:, a * P:(a + 1) * P], xin[:, par, a * D:(a + 1) * D], ident[:, :])
                mm.then_inc(d.turned, 1)

            pe.wait_ge(weights_ready, NW // 4 + 2)

            def wx_step(j, par):
                g = 2 * j + par
                turn_rows(p_wx, j, par)
                pe.wait_ge(p_wx.copied, g + 1)
                pe.wait_ge(p_wx.rows, g)
                for a in range(A):
                    o = bank[2 + par][:, a * D:(a + 1) * D]
                    pe.matmul(o, xT[:, par, a * P:(a + 1) * P], wT[:, W_0, :], start=True, stop=False)
                    mm = pe.matmul(o, ones_f[0:1, :], b0_row[:, :], start=False, stop=True)
                mm.then_inc(p_wx.prod, 1)
            groups(pe, wx_step)
            sort_sums(1)

            def sums(ph, by_node=False, features=False):
                with pe.Fori(0, TURNS) as t:
                    for q in range(NQ):
                        pe.wait_ge(hot_ready[q], ph * TURNS + t + 1)
                        if features:
                            pe.wait_ge(attr_in[q], 32 * STURNS + 16 * FULLTURNS + (t + 1) * 16)
                        for u in range(q * 4, q * 4 + 4):
                            k = u % 4
                            pe.wait_ge(slot_dma[u], (2 * STURNS + ph * TURNS + t + 1) * 16)
                            lhs, rhs = (hot, msg) if by_node else (msg, hot)
                            if features:
                                pe.matmul(bank[4 + q][0:DE + 1, k * P:(k + 1) * P], rec[:, u, 0:DE + 1], hot[:, u, :],
                                          start=True, stop=True)
                            mm = pe.matmul(bank[q][:, k * P:(k + 1) * P], lhs[:, u, :], rhs[:, u, :],
                                           start=True, stop=True)
                        mm.then_inc(summed[q], 1)
                pe.wait_ge(added, (ph + 1) * NCH)
                if features:
                    pe.wait_ge(feat_added, NCH)

            sums(0, by_node=True)
            sums(1, features=True)

            def l1_step(j, par):
                g = 2 * j + par
                turn_rows(p_l1, j, par)
                pe.wait_ge(p_l1.copied, g + 1)
                pe.wait_ge(p_l1.free, g + 1)
                for a in range(A):
                    o = bank[2 + par][:, a * D:(a + 1) * D]
                    pe.matmul(o, xT[:, par, a * P:(a + 1) * P], w2a[:, :], start=True, stop=False)
                    pe.matmul(o, accs[:, par, a * P:(a + 1) * P], c1[:, :], start=False, stop=False)
                    pe.matmul(o, auxs[0:DE + 1, par, a * P:(a + 1) * P], c2[:, :], start=False, stop=True)
                    mm = pe.matmul(bank[4 + par][:, a:a + 1], auxs[0:DE + 1, par, a * P:(a + 1) * P], deg_pick[:, :],
                                   start=True, stop=True)
                mm.then_inc(p_l1.prod, 1)
            groups(pe, l1_step)

            def l2_steps(d, wl, wr, loads):
                def step(j, par):
                    g = 2 * j + par
                    turn_rows(d, j, par, loads)
                    pe.wait_ge(d.copied, g + 1)
                    pe.wait_ge(d.free, g + 1)
                    for a in range(A):
                        pe.matmul(bank[2 + par][:, a * D:(a + 1) * D], accs[:, par, a * P:(a + 1) * P], wT[:, wl, :],
                                  start=True, stop=True)
                        mm = pe.matmul(bank[4 + par][:, a * D:(a + 1) * D], xT[:, par, a * P:(a + 1) * P], wT[:, wr, :],
                                       start=True, stop=True)
                    mm.then_inc(d.prod, 1)
                groups(pe, step)
            sums(2)
            l2_steps(p_l2a, W_1L, W_1R, 1)
            sums(3)
            l2_steps(p_l2b, W_2L, W_2R, 2)

            def types(n, g):
                for a in range(A):
                    if a % 2 == 0:
                        if n > 0 or not isinstance(g, int) or g > 0:
                            pe.wait_ge(t_rows[a // 2], n * NG + g)
                    mm = pe.matmul(bank[2 + a][:, :], auxs[:, 0, a * P:(a + 1) * P],
                                   wT[:, W_ET:W_ET + KT, :].rearrange("p k f -> p (k f)"), start=True, stop=True)
                    if a % 2:
                        mm.then_inc(t_prod[a // 2], 1)

            def t_step(j, par):
                g = 2 * j + par
                turn_rows(p_t, j, par)
                pe.wait_ge(p_t.copied, g + 1)
                types(0, g)
            groups(pe, t_step)

            def gates(n, g):
                pe.wait_ge(h_ready, n * NG + g)
                a, h = cols(acc, g * GN, GN), cols(aux, g * GN, GN)
                for c in range(2):
                    pe.matmul(bank[c][:, :], wT[:, W_IH + c, :], a, start=True, stop=False)
                    pe.matmul(bank[c][:, :], wT[:, W_HH + c, :], h, start=False, stop=True)
                pe.matmul(bank[6][:, :], wT[:, W_IH + 2, :], a, start=True, stop=True)
                pe.matmul(bank[7][:, :], wT[:, W_HH + 2, :], h, start=True, stop=True).then_inc(gate_prod, 1)

            for n in range(3):
                sums(4 + n)
                if n < 2:
                    gates(n, 0)
                    with pe.Fori(1, NG) as g:
                        gates(n, g)
                        pe.wait_ge(h_copied, n * NG + g)
                        types(n + 1, g - 1)
                    pe.wait_ge(h_copied, (n + 1) * NG)
                    types(n + 1, NG - 1)
                else:
                    with pe.Fori(0, NG) as g:
                        gates(n, g)

            pe.wait_ge(h_ready, 3 * NG)

            def fin_step(j, par):
                g = 2 * j + par
                turn_rows(p_fin, j, par)
                pe.wait_ge(p_fin.copied, g + 1)
                h = cols(aux, g * GN, GN)
                pe.matmul(bank[2][:, :], wT[:, W_I, :], h, start=True, stop=False)
                pe.matmul(bank[2][:, :], wT[:, W_I + 1, :], xT[:, par, :], start=False, stop=True)
                pe.matmul(bank[3][:, :], wT[:, W_J, :], h, start=True, stop=True).then_inc(p_fin.prod, 1)
                pe.wait_ge(p_fin.free, g + 1)
                for a in range(A):
                    mm = pe.transpose(bank[4 + par][:, a * P:(a + 1) * P], y[:, a * P:(a + 1) * P], ident[:, :])
                mm.then_inc(t_prod[0], 1)
            groups(pe, fin_step)

        @block.vector
        def _(v):
            class Chain:
                base = per = k = 0
                g = 0

                def link(self, ins):
                    self.k += 1
                    ins.then_inc(chain, 1)
                    v.wait_ge(chain, self.base + self.g * self.per + self.k)

                def loop(self, g, per):
                    self.g, self.per, self.k = g, per, 0

                def end(self, turns):
                    assert not self.per or self.k == self.per, (self.k, self.per)
                    self.base += turns * self.per if self.per else self.k
                    self.g = self.per = self.k = 0
            ch = Chain()
            link = ch.link

            v.memset(s_key.bitcast(I32)[96:P, ETAIL:EC], -1).then_inc(tails_set, 1)
            v.memset(d_key.bitcast(I32)[96:P, ETAIL:EC], -1).then_inc(tails_set, 1)
            v.memset(meta_w[96:P, ETAIL:EC], 0.0).then_inc(tails_set, 1)
            v.memset(meta_low[:, 0:EC].bitcast(I32)[96:P, ETAIL:EC], 0).then_inc(tails_set, 1)
            v.wait_ge(const_ready, 1)
            v.tensor_copy(iota_f[:, :], iota_i[:, :])
            link(v.tensor_copy(chunk_f[:, :], chunk_i[:, :]))

            def places(key, tile, low):
                a, b = s_mask.bitcast(I32), s_scan.bitcast(I32)
                v.tensor_scalar(a, key, 9, None, ALU.arith_shift_right)
                link(v.tensor_scalar(b, key, A - 1, None, ALU.bitwise_and))
                link(v.scalar_tensor_tensor(out=tile, in0=a, scalar=float(A), in1=b, op0=ALU.mult, op1=ALU.add))
                link(v.tensor_scalar(a, key, 2, P - 1, ALU.arith_shift_right, ALU.bitwise_and))
                link(v.tensor_copy(low, a))

            def count(tile):
                ch.end(1)
                with v.Fori(0, NT) as t:
                    ch.loop(t, 1)
                    link(v.tensor_scalar(s_mask, tile, iota_f[:, bass.ds(t, 1)], 0.0, ALU.is_equal, ALU.add,
                                         accum_out=hist[:, bass.ds(t, 1)]))
                ch.end(NT)
                link(v.memset(spare[:, :], 0.0))
                v.sem_inc(hist_ready, 1)

            def starts(n):
                v.wait_ge(base_sums, n + 1)
                link(v.tensor_scalar(cnt_i[:, :], bank[6][:, P:P + NT], float(P - 1), None, ALU.add))
                link(v.tensor_scalar(cnt_i[:, :], cnt_i[:, :], 7, None, ALU.arith_shift_right))
                link(v.tensor_copy(cnt_f[:, :], cnt_i[:, :]))
                link(v.tensor_tensor_scan(cum[:, :], cnt_f[:, :], cnt_f[:, :], 0.0, ALU.add, ALU.max))
                link(v.tensor_tensor(spare[:, :], cum[:, :], cnt_f[:, :], ALU.subtract))
                link(v.scalar_tensor_tensor(out=base[:, :], in0=spare[:, :], scalar=float(P), in1=bank[6][:, 0:NT],
                                            op0=ALU.mult, op1=ALU.add))
                for c in range(IPC):
                    link(v.tensor_scalar(spare[:, :], cum[:, :], chunk_f[:, c:c + 1], 0.0, ALU.is_le, ALU.add,
                                         accum_out=tid[:, c:c + 1]))
                if n:
                    v.wait_ge(off_out, 16 * n)
                v.tensor_scalar(tid_i[:, :], tid[:, :], float(NT - 1), float(P), ALU.min, ALU.mult).then_inc(off_ready, 1)

            def positions(n, tile, pos):
                link(v.memset(pos, FAR))
                ch.end(1)
                with v.Fori(0, NT) as t:
                    ch.loop(t, 3)
                    link(v.tensor_scalar(s_mask, tile, iota_f[:, bass.ds(t, 1)], None, ALU.is_equal))
                    link(v.tensor_tensor_scan(s_scan, s_mask, s_mask, base[:, bass.ds(t, 1)], ALU.add, ALU.max))
                    v.sem_inc(vec_seen, 1)
                    link(v.copy_predicated(pos, s_mask.bitcast(U32), s_scan))
                ch.end(NT)
                a, b = s_mask.bitcast(I32), s_scan.bitcast(I32)
                link(v.tensor_scalar(a, pos, -1.0, None, ALU.add))
                link(v.tensor_scalar(b, a, P - 1, None, ALU.bitwise_and))
                link(v.tensor_scalar(a, a, 7, None, ALU.arith_shift_right))
                v.scalar_tensor_tensor(out=pos, in0=b, scalar=float(NCH), in1=a, op0=ALU.mult,
                                       op1=ALU.add).then_inc(pos_ready, 1)
                v.wait_ge(pos_ready, n + 1)

            si, di = s_key.bitcast(I32), d_key.bitcast(I32)
            v.wait_ge(keys_in, 16 * 12)
            places(si, s_tile, s_rec[:, :, 1])
            count(s_tile)
            v.tensor_copy(s_rec[:, :, 0], di)
            link(v.tensor_tensor(s_mask, si, di, ALU.not_equal))
            link(v.tensor_tensor(s_scan, meta_w[:, 0:EC], meta_w[:, 0:EC], ALU.mult))
            link(v.tensor_tensor(s_rec[:, :, 2], s_mask, s_scan, ALU.mult))
            starts(0)
            positions(0, s_tile, s_pos)
            v.memset(d_rec[:, :, 0], 1.0)
            v.tensor_copy(d_rec[:, :, 2], meta_w[:, 0:EC])
            v.tensor_copy(d_rec[:, :, 3], si)
            v.scalar_tensor_tensor(out=d_rec[:, :, 4], in0=si, scalar=float(KT), in1=meta_low[:, 0:EC].bitcast(I32),
                                   op0=ALU.mult, op1=ALU.add)
            places(di, d_tile, d_rec[:, :, 1])
            count(d_tile)
            starts(1)
            positions(1, d_tile, d_pos)
            ch.end(1)

            def gather_steps(ph, index, low, weight, features=False):
                link(v.memset(acc[:, :], 0.0))
                if features:
                    link(v.memset(aux[0:DE + 1, :], 0.0))
                ch.end(1)

                def add(t, u, off):
                    n = ph * NCH + t * U + u
                    if not isinstance(n, int) or n > 0:
                        v.wait_ge(added, n)
                    into = acc[:, bass.ds(off, P)]
                    k = u % 4
                    ins = v.tensor_tensor(into, into, bank[u // 4][:, k * P:(k + 1) * P], ALU.add)
                    ins.then_inc(added, 1)
                    if features:
                        m = t * U + u
                        if not isinstance(m, int) or m > 0:
                            v.wait_ge(feat_added, m)
                        into = aux[0:DE + 1, bass.ds(off, P)]
                        v.tensor_tensor(into, into, bank[4 + u // 4][0:DE + 1, k * P:(k + 1) * P],
                                        ALU.add).then_inc(feat_added, 1)

                def offsets(t):
                    src_ = tile_off[0:1, t * U:(t + 1) * U] if isinstance(t, int) else tile_off[0:1, bass.ds(t * U, U)]
                    return nc.values_load_multi_w_load_instructions(
                        src_, engines=[mybir.EngineType.DVE], min_val=0, max_val=(NT - 1) * P,
                        skip_runtime_bounds_check_because="the kernel writes 128 times a tile number, at most NT - 1")[1]

                def turn(t, first=False):
                    if not first:
                        off = offsets(t - 1)
                    for q in range(NQ):
                        if not first:
                            v.wait_ge(summed[q], ph * TURNS + t)
                        c = t * U + q * 4
                        v.tensor_copy(stage[:, q * 4:q * 4 + 4], index(c, 4)).then_inc(staged[q], 1)
                        for u in range(q * 4, q * 4 + 4):
                            if not first:
                                add(t - 1, u, off[u])
                            ins = v.tensor_scalar(hot[:, u, :], iota_f[:, :], low(c + u % 4),
                                                  weight(c + u % 4) if weight else None, ALU.is_equal,
                                                  ALU.mult if weight else ALU.bypass)
                        ins.then_inc(hot_ready[q], 1)

                turn(0, first=True)
                with v.Fori(1, TURNS) as t:
                    turn(t)
                off = offsets(TURNS - 1)
                for q in range(NQ):
                    v.wait_ge(summed[q], (ph + 1) * TURNS)
                    for u in range(q * 4, q * 4 + 4):
                        add(TURNS - 1, u, off[u])
                v.wait_ge(added, (ph + 1) * NCH)
                if features:
                    v.wait_ge(feat_added, NCH)

            def norm(d, j, par):
                g = 2 * j + par
                for a in range(A):
                    ins = v.bn_stats(stats[:, a, :], z[:, a * D:(a + 1) * D])
                link(ins)
                v.sem_inc(vec_seen, 1)
                for a in range(A):
                    ins = v.bn_aggr(mv[:, a, :], stats[:, a, :])
                ins.then_inc(d.var, 1)
                v.wait_ge(d.std, g + 1)
                link(v.reciprocal(rstd[:, :], std[:, :]))
                v.wait_ge(d.st[par], j * 16)
                for a in range(A):
                    ins = v.tensor_scalar(res[:, par, a * D:(a + 1) * D], z[:, a * D:(a + 1) * D], mv[:, a, 0:1],
                                          rstd[:, a:a + 1], ALU.subtract, ALU.mult)
                ins.then_inc(d.rows, 1)

            for u in range(U):
                v.wait_ge(slot_dma[u], 16 * 2 * STURNS)
            v.wait_ge(srcmeta_in, 16)
            v.wait_ge(off_in, 16)
            gather_steps(0, lambda c, n: srcmeta[:, c:c + n, 0] if isinstance(c, int) else srcmeta[:, bass.ds(c, n), 0],
                         lambda c: cols(aux[:, 0:RS * NCH], c * RS + 1, 1),
                         lambda c: cols(aux[:, 0:RS * NCH], c * RS + 2, 1))

            def l0_step(j, par):
                g = 2 * j + par
                ch.loop(g, 4)
                v.wait_ge(p_l0.ld[par], (j + 1) * 32)
                v.wait_ge(p_l0.rows, g)
                link(v.tensor_tensor(z[:, :], yin[:, par, :], cols(acc, g * GN, GN), ALU.mult))
                link(v.tensor_tensor(z[:, :], z[:, :], xin[:, par, :], ALU.add))
                norm(p_l0, j, par)
            groups(v, l0_step)
            ch.end(NG)

            v.wait_ge(block_read, NBLK)
            v.wait_ge(off_in, 32)
            src_of = lambda c, n: cols(meta_src, c, n)
            low_of = lambda c: cols(meta_low, c, 1)
            weight_of = lambda c: cols(meta_w, c, 1)
            gather_steps(1, src_of, low_of, None, features=True)
            v.sem_inc(p_l1.free, 2)

            def l1_step(j, par):
                g = 2 * j + par
                ch.loop(g, 7)
                v.wait_ge(p_l1.prod, g + 1)
                v.wait_ge(p_l1.rows, g)
                v.tensor_scalar(cnt_f[:, 0:A], bank[4 + par][:, 0:A], 1.0, None, ALU.max)
                link(v.tensor_tensor(z[:, :], bank[2 + par][:, :], xin[:, par, :], ALU.add))
                v.sem_inc(p_l1.free, 1)
                link(v.tensor_tensor(cnt_f[:, A:2 * A], cnt_f[:, 0:A], cnt_f[:, 0:A], ALU.mult))
                link(v.reciprocal(cols(rdeg, g * A, A), cnt_f[:, A:2 * A]))
                link(v.tensor_tensor(z[:, :], z[:, :], b2_all[:, :], ALU.add))
                norm(p_l1, j, par)
                link(v.memset(cnt_f[:, 0:A], 0.0))
            groups(v, l1_step)
            ch.end(NG)

            def combine(d, par, g):
                for a in range(A):
                    ins = v.tensor_scalar(z[:, a * D:(a + 1) * D], bank[2 + par][:, a * D:(a + 1) * D],
                                          cols(rdeg, g * A + a, 1), None, ALU.mult)
                link(ins)
                link(v.tensor_tensor(z[:, :], z[:, :], bank[4 + par][:, :], ALU.add))
                v.sem_inc(d.free, 1)

            gather_steps(2, src_of, low_of, weight_of)
            v.sem_inc(p_l2a.free, 2)

            def l2a_step(j, par):
                g = 2 * j + par
                ch.loop(g, 2)
                v.wait_ge(p_l2a.prod, g + 1)
                v.wait_ge(p_l2a.rows, g)
                combine(p_l2a, par, g)
                v.wait_ge(p_l2a.st[par], j * 16)
                v.tensor_scalar(res[:, par, :], z[:, :], 0.0, None, ALU.max).then_inc(p_l2a.rows, 1)
            groups(v, l2a_step)
            ch.end(NG)
            gather_steps(3, src_of, low_of, weight_of)
            v.sem_inc(p_l2b.free, 2)

            def l2b_step(j, par):
                g = 2 * j + par
                ch.loop(g, 5)
                v.wait_ge(p_l2b.prod, g + 1)
                v.wait_ge(p_l2b.rows, g)
                combine(p_l2b, par, g)
                link(v.tensor_tensor(z[:, :], z[:, :], yin[:, par, :], ALU.add))
                norm(p_l2b, j, par)
            groups(v, l2b_step)
            ch.end(NG)

            def t_add(n, g):
                for hh in range(2):
                    v.wait_ge(t_prod[hh], n * NG + g + 1)
                    if n > 0 or not isinstance(g, int) or g > 0:
                        v.wait_ge(t_out[hh], (n * NG + g) * 16)
                    for a in range(2):
                        ins = v.tensor_tensor(wide[:, hh, a * KT * D:(a + 1) * KT * D], bank[2 + 2 * hh + a][:, :],
                                              bet_all[:, :], ALU.add)
                    ins.then_inc(t_rows[hh], 1)

            with v.Fori(0, NG) as g:
                t_add(0, g)

            def gru(n, g):
                i = n * NG + g
                h = cols(aux, g * GN, GN)
                v.wait_ge(gate_rz, i + 1)
                link(v.scalar_tensor_tensor(out=z[:, :], in0=bank[7][:, :], scalar=gru_b[:, 5:6], in1=xT[:, 0, :],
                                            op0=ALU.add, op1=ALU.mult))
                v.tensor_tensor(y[:, :], z[:, :], bank[6][:, :], ALU.add).then_inc(gate_pre, 1)
                v.wait_ge(gate_n, i + 1)
                link(v.tensor_tensor(z[:, :], h, yin[:, 0, :], ALU.subtract))
                link(v.tensor_tensor(z[:, :], z[:, :], xT[:, 1, :], ALU.mult))
                v.tensor_tensor(h, z[:, :], yin[:, 0, :], ALU.add).then_inc(h_ready, 1)

            for n in range(3):
                gather_steps(4 + n, lambda c, k: cols(meta_row, c, k), low_of, None)
                if n < 2:
                    gru(n, 0)
                    ch.end(1)
                    with v.Fori(1, NG) as g:
                        ch.loop(g - 1, 3)
                        gru(n, g)
                        t_add(n + 1, g - 1)
                    ch.end(NG - 1)
                    t_add(n + 1, NG - 1)
                else:
                    with v.Fori(0, NG) as g:
                        ch.loop(g, 3)
                        gru(n, g)
                    ch.end(NG)

            def fin_step(j, par):
                g = 2 * j + par
                ch.loop(g, 3)
                v.wait_ge(gate_rz, 3 * NG + g + 1)
                v.wait_ge(p_fin.rows, g)
                v.scalar_tensor_tensor(out=y[:, :], in0=bank[3][:, :], scalar=jb_col[:, 0:1], in1=yin[:, par, :],
                                       op0=ALU.add, op1=ALU.mult).then_inc(p_fin.free, 1)
                v.wait_ge(t_prod[0], 3 * NG + g + 1)
                link(v.tensor_tensor(z[:, :], bank[4 + par][:, :], xin[:, par, :], ALU.add))
                norm(p_fin, j, par)
            groups(v, fin_step)


_INS = ['x', 'src', 'dst', 'edge_attr_32', 'edge_type_4', 'edge_weight', 'L0_gnn_W', 'L0_gnn_b', 'L1_gnn_u', 'L1_gnn_W1',
        'L1_gnn_b1', 'L1_gnn_W2', 'L1_gnn_b2', 'L2_gnn_W1l', 'L2_gnn_W1r', 'L2_gnn_W2l', 'L2_gnn_W2r', 'L3_gnn_W_et',
        'L3_gnn_b_et', 'L3_gnn_W_ih', 'L3_gnn_b_ih', 'L3_gnn_W_hh', 'L3_gnn_b_hh', 'L3_gnn_i_w', 'L3_gnn_i_b',
        'L3_gnn_j_w', 'L3_gnn_j_b']


def kernel(**inputs):
    import numpy as _np
    import concourse.bacc as _bacc
    from concourse import mybir as _mybir
    from concourse.bass_utils import run_bass_kernel_spmd as _run

    nc = _bacc.Bacc("TRN2", target_bir_lowering=False, num_devices=1)
    arrays, args = {}, []
    for name in _INS:
        a = _np.ascontiguousarray(inputs[name])
        arrays[f"in_{name}"] = a
        args.append(nc.dram_tensor(f"in_{name}", a.shape, _mybir.dt.from_np(a.dtype), kind="ExternalInput").ap())
    o = nc.dram_tensor("out_0", (N, D), F32, kind="ExternalOutput").ap()
    build(nc, *args, o)
    r = _run(nc, [arrays], core_ids=[0])
    return r.results[0]["out_0"]
```

```python
from contextlib import ExitStack

import concourse.bass as bass
from concourse import mybir

F32 = mybir.dt.float32
I32 = mybir.dt.int32
U32 = mybir.dt.uint32
U16 = mybir.dt.uint16
BF16 = mybir.dt.bfloat16
ALU = mybir.AluOpType
ACT = mybir.ActivationFunctionType

P = 128
D = 128
DE = 32
KT = 4
N = 12500
E = 200000
A = 4
GN = A * P
NG = -(-N // GN)
NT = NG * A
NPAD = NG * GN
U = 16
NQ = 4
EC = U * -(-E // (P * U))
ETAIL = E - (P - 1) * EC
STURNS = EC // U
FULLTURNS = ETAIL // U
NCH = U * -(-((E + (P - 1) * NT) // P) // U)
TURNS = NCH // U
IPC = NCH // P
RS = 3
RD = 4
ZS = NCH // 8
LAST_OUTS = -(-(N - (NG - 1) * GN) // P)
FIRST = 2
EPS = 1e-5
FAR = float(2 ** 20)
NW = 20
W_0, W_1L, W_1R, W_2L, W_2R, W_ET, W_IH, W_HH, W_I, W_J, W_1A, W_1B = 0, 1, 2, 3, 4, 5, 9, 12, 15, 17, 18, 19
WEIGHT_DMAS = NW + 1 + 3 + A + KT + 4
assert ETAIL % U == 0 and NCH % P == 0 and NG % 2 == 1 and (NPAD - N) * D % P == 0
assert ((P - 1) * NCH + ((int(FAR) - 1) >> 7)) >= P * NCH


def build(nc, x, src, dst, edge_attr_32, edge_type_4, edge_weight, L0_gnn_W, L0_gnn_b, L1_gnn_u, L1_gnn_W1,
          L1_gnn_b1, L1_gnn_W2, L1_gnn_b2, L2_gnn_W1l, L2_gnn_W1r, L2_gnn_W2l, L2_gnn_W2r, L3_gnn_W_et,
          L3_gnn_b_et, L3_gnn_W_ih, L3_gnn_b_ih, L3_gnn_W_hh, L3_gnn_b_hh, L3_gnn_i_w, L3_gnn_i_b, L3_gnn_j_w,
          L3_gnn_j_b, out):
    ctx = ExitStack()
    with ctx:
        def sb(name, shape, dt=F32):
            return ctx.enter_context(nc.sbuf_tensor(name, shape, dt))

        def sem(name):
            return ctx.enter_context(nc.semaphore(name))

        def dram(name, shape, dt=F32):
            return nc.dram_tensor(name, shape, dt, kind="Internal").ap()

        X0 = dram("t_x0", [NPAD, D])
        WX = dram("t_wx", [NPAD, D])
        X1 = dram("t_x1", [NPAD, D])
        X2 = dram("t_x2", [NPAD, D])
        H1 = dram("t_h1", [NPAD, D])
        X3 = dram("t_x3", [NPAD, D])
        TT = dram("t_types", [NPAD, KT * D])
        SRC_REC = dram("src_records", [P * NCH, RS])
        DST_REC = dram("dst_records", [E + P, RD])
        DST_ATTR = dram("dst_attributes", [E + P, DE])
        SRC_OFF = dram("src_tile_offsets", [NCH], I32)
        DST_OFF = dram("dst_tile_offsets", [NCH], I32)
        DST_NODE = dram("dst_first_nodes", [NCH])
        DST_FIRST = dram("dst_first_records", [NCH], I32)

        acc = sb("acc", [P, NT * P])
        aux = sb("aux", [P, NT * P])
        meta_low = sb("meta_low", [P, NCH])
        meta_w = sb("meta_w", [P, NCH])
        meta_src = sb("meta_src", [P, NCH], U16)
        meta_row = sb("meta_row", [P, NCH], U16)
        chunk_at = sb("chunk_at", [2, NCH], I32)
        tile_off = chunk_at[0:1, :]
        first_rec = chunk_at[1:2, :]
        unsorted = sb("unsorted", [1, 1], I32)
        ring = sb("ring", [P, 2 * U, P])
        msg, hot = ring[:, 0:U, :], ring[:, U:2 * U, :]
        stage = sb("stage", [P, U], U32)
        rec = sb("rec", [P, U, DE + 1])
        drec = sb("drec", [P, U, RD])
        srec = sb("srec", [P, U, RS])
        wT = sb("wT", [P, NW, P])
        w2a = sb("w2a", [P, D])
        w2b = sb("w2b", [P, D])
        c1 = sb("c1", [P, D])
        c2 = sb("c2", [DE + 1, D])
        b0_row = sb("b0_row", [1, D])
        b2_all = sb("b2_all", [P, GN])
        bet_all = sb("bet_all", [P, KT * D])
        gru_b = sb("gru_b", [P, 6])
        gru_rz = sb("gru_rz", [P, 2])
        ib_col = sb("ib_col", [P, 1])
        jb_col = sb("jb_col", [P, 1])
        eps_col = sb("eps_col", [P, 1])
        ones_f = sb("ones_f", [P, P])
        ident = sb("ident", [P, P])
        before = sb("before", [P, P])
        iota_i = sb("iota_i", [P, P], I32)
        iota_f = sb("iota_f", [P, P])
        chunk_i = sb("chunk_i", [P, IPC], I32)
        chunk_f = sb("chunk_f", [P, IPC])
        deg_pick = sb("deg_pick", [DE + 1, 1])
        hist = sb("hist", [P, NT])
        hist0 = sb("hist0", [P, NT])
        base = sb("base", [P, NT])
        cnt_i = sb("cnt_i", [P, NT], I32)
        cnt_f = sb("cnt_f", [P, NT])
        cum = sb("cum", [P, NT])
        spare = sb("spare", [P, NT])
        tid = sb("tid", [P, IPC])
        tid_i = sb("tid_i", [P, IPC], I32)
        node = sb("node", [P, IPC])
        shift = sb("shift", [P, IPC])
        first_i = sb("first_i", [P, IPC], I32)
        pads = sb("pads", [P, NT])
        falls = sb("falls", [P, 1])
        empty_rec = sb("empty_rec", [P, RD])
        rdeg = sb("rdeg", [P, NT])
        xin = sb("xin", [P, 2, GN])
        yin = sb("yin", [P, 2, GN])
        xT = sb("xT", [P, 2, GN])
        accs = sb("accs", [P, 2, GN])
        auxs = sb("auxs", [P, 2, GN])
        z = sb("z", [P, 2, GN])
        y = sb("y", [P, GN])
        res = sb("res", [P, 2, GN])
        wide = sb("wide", [P, 2, 2 * KT * D])
        stats = sb("stats", [P, A, 6])
        mv = sb("mv", [P, 2, A, 2])
        std = sb("std", [P, 2, A])
        rstd = sb("rstd", [P, 2, A])

        def part(t, k, n=1, dt=None):
            v = t[:, k * EC:(k + n) * EC]
            return v if dt is None else v.bitcast(dt)
        s_key, s_tile, s_mask, s_scan, s_pos = (part(acc, k) for k in range(5))
        s_tile = s_tile.bitcast(BF16)[:, 0:EC]
        s_rec = part(acc, 5, RS).rearrange("p (e w) -> p e w", w=RS)
        d_key, d_tile, d_pos = (part(aux, k) for k in range(3))
        d_tile = d_tile.bitcast(BF16)[:, 0:EC]
        d_rec = part(aux, 3, RD).rearrange("p (e w) -> p e w", w=RD)
        srcmeta = aux[:, 0:RS * NCH].rearrange("p (c w) -> p c w", w=RS)
        dstmeta = aux[:, NT * P - RD * NCH:NT * P].rearrange("p (c w) -> p c w", w=RD)
        chunk_node = wide[:, :, :].rearrange("p a b -> p (a b)")[:, 0:NCH]
        zero_src = yin[:, :, :].rearrange("p a b -> p (a b)")[:, 0:ZS * RS]

        bank = [ctx.enter_context(nc.psum_tensor(f"bank{i}", [P, 512], F32)) for i in range(8)]

        tails_set = sem("tails_set")
        zeros_set = sem("zeros_set")
        x0_out = sem("x0_out")
        feat_added = sem("feat_added")
        const_ready = sem("const_ready")
        pool_const = sem("pool_const")
        weights_in = sem("weights_in")
        weights_turned = sem("weights_turned")
        weights_ready = sem("weights_ready")
        keys_in = sem("keys_in")
        next_in = sem("next_in")
        falls_ready = sem("falls_ready")
        falls_summed = sem("falls_summed")
        order_known = sem("order_known")
        empty_out = sem("empty_out")
        sorted_out = sem("sorted_out")
        records_in = [sem(f"records_in{q}") for q in range(NQ)]
        nodes_in = sem("nodes_in")
        fields_ready = sem("fields_ready")
        sort_staged = [sem(f"sort_staged{q}") for q in range(NQ)]
        sort_attr = [sem(f"sort_attr{q}") for q in range(NQ)]
        sort_dma = [sem(f"sort_dma{q}") for q in range(NQ)]
        zeros_out = sem("zeros_out")
        chain = sem("chain")
        hist_ready = sem("hist_ready")
        base_sums = sem("base_sums")
        pos_ready = sem("pos_ready")
        off_ready = sem("off_ready")
        off_out = sem("off_out")
        off_in = sem("off_in")
        srcmeta_in = sem("srcmeta_in")
        staged = [sem(f"staged{q}") for q in range(NQ)]
        attr_in = [sem(f"attr_in{q}") for q in range(NQ)]
        slot_dma = [sem(f"slot_dma{u}") for u in range(U)]
        hot_ready = [sem(f"hot_ready{q}") for q in range(NQ)]
        summed = [sem(f"summed{q}") for q in range(NQ)]
        added = sem("added")
        pool_seen = sem("pool_seen")
        vec_seen = sem("vec_seen")

        class Dense:
            def __init__(self, name, prod=True, norm=True, out_=True):
                self.ld = [sem(f"{name}_in{i}") for i in range(2)]
                if prod:
                    self.turned = sem(f"{name}_turned")
                    self.copied = sem(f"{name}_copied")
                    self.prod = sem(f"{name}_prod")
                if prod and name != "wx":
                    self.free = sem(f"{name}_free")
                if norm:
                    self.var = sem(f"{name}_var")
                    self.std = sem(f"{name}_std")
                if out_:
                    self.rows = sem(f"{name}_rows")
                    self.st = [sem(f"{name}_out{i}") for i in range(2)]

        p_wx, p_l2a = (Dense(n, norm=False) for n in ("wx", "l2a"))
        p_l0 = Dense("l0", prod=False)
        p_l1, p_l2b, p_fin = (Dense(n) for n in ("l1", "l2b", "fin"))
        p_t = Dense("tt", norm=False, out_=False)
        gate_prod = sem("gate_prod")
        gate_rz = sem("gate_rz")
        gate_pre = sem("gate_pre")
        gate_n = sem("gate_n")
        h_ready = sem("h_ready")
        h_copied = sem("h_copied")
        gate_nprod = sem("gate_nprod")
        out_turned = sem("out_turned")
        t_prod = [sem(f"t_prod{i}") for i in range(2)]
        t_rows = [sem(f"t_rows{i}") for i in range(2)]
        t_out = [sem(f"t_out{i}") for i in range(2)]


        def rows(t, g):
            v = t[g * GN:(g + 1) * GN, :] if isinstance(g, int) else t[bass.ds(g * GN, GN), :]
            return v.rearrange("(a p) f -> p a f", a=A)

        def by_tile(slot, n=A):
            return slot.rearrange("p (a f) -> p a f", a=n)

        def loaded(eng, src_, n, top, why):
            return nc.values_load_multi_w_load_instructions(src_, engines=[eng], min_val=0, max_val=top,
                                                            skip_runtime_bounds_check_because=why)[1]

        def is_unsorted(eng):
            return loaded(eng, unsorted[0:1, 0:1], 1, 1, "the kernel writes 0 or 1")[0] > 0

        def groups(eng, step):
            for j in range(FIRST):
                step(j, 0)
                step(j, 1)
            with eng.Fori(FIRST, NG // 2) as j:
                step(j, 0)
                step(j, 1)
            step(NG // 2, 0)

        def wait(eng, s_, n):
            if not isinstance(n, int) or n > 0:
                eng.wait_ge(s_, n)

        def is_last(g):
            return isinstance(g, int) and g == NG - 1

        def cols(t, start, n):
            return t[:, start:start + n] if isinstance(start, int) else t[:, bass.ds(start, n)]

        block = ctx.enter_context(nc.Block())

        @block.sync
        def _(sp):
            def edges_in(tile, a):
                v = a[0:(P - 1) * EC].rearrange("(p e) -> p e", e=EC)
                for lo, hi in ((0, 112), (112, P - 1)):
                    sp.dma_start(tile[lo:hi, :], v[lo:hi, :]).then_inc(keys_in, 16)
                sp.dma_start(tile[P - 1:P, 0:ETAIL], a[(P - 1) * EC:E].rearrange("(p e) -> p e", p=1)).then_inc(keys_in, 16)

            sp.wait_ge(tails_set, 5)
            edges_in(s_key.bitcast(I32), src)
            edges_in(d_key.bitcast(I32), dst)
            edges_in(meta_w[:, 0:EC], edge_weight)
            edges_in(meta_low[:, 0:EC].bitcast(I32), edge_type_4)
            after = d_pos.bitcast(I32)
            v = dst[1:(P - 1) * EC + 1].rearrange("(p e) -> p e", e=EC)
            for lo, hi in ((0, 112), (112, P - 1)):
                sp.dma_start(after[lo:hi, :], v[lo:hi, :]).then_inc(next_in, 16)
            sp.dma_start(after[P - 1:P, 0:ETAIL - 1],
                         dst[(P - 1) * EC + 1:E].rearrange("(p e) -> p e", p=1)).then_inc(next_in, 16)

            w_in = [L0_gnn_W, L2_gnn_W1l, L2_gnn_W1r, L2_gnn_W2l, L2_gnn_W2r]
            w_in += [L3_gnn_W_et[k] for k in range(KT)]
            w_in += [w[c * D:(c + 1) * D, :] for w in (L3_gnn_W_ih, L3_gnn_W_hh) for c in range(3)]
            w_in += [L3_gnn_i_w[:, 0:D], L3_gnn_i_w[:, D:2 * D], L3_gnn_j_w, L1_gnn_W1[0:D, :]]
            for i, w in enumerate(w_in):
                sp.dma_start(ring[:, i, :], w).then_inc(weights_in, 16)
            sp.dma_start(ring[0:DE, NW - 1, :], L1_gnn_W1[D:D + DE, :]).then_inc(weights_in, 16)
            sp.dma_start(ring[DE:DE + 1, NW - 1, :], L1_gnn_b1.rearrange("(a d) -> a d", a=1)).then_inc(weights_in, 16)
            sp.dma_start(w2a[:, :], L1_gnn_W2[0:D, :]).then_inc(weights_in, 16)
            sp.dma_start(w2b[:, :], L1_gnn_W2[D:2 * D, :]).then_inc(weights_in, 16)
            sp.dma_start(b0_row[:, :], L0_gnn_b.rearrange("(a d) -> a d", a=1)).then_inc(weights_in, 16)
            for a in range(A):
                sp.dma_start(b2_all[:, a * D:(a + 1) * D],
                             L1_gnn_b2.rearrange("(a d) -> a d", a=1).to_broadcast([P, D])).then_inc(weights_in, 16)
            for k in range(KT):
                sp.dma_start(bet_all[:, k * D:(k + 1) * D],
                             L3_gnn_b_et[k:k + 1, :].to_broadcast([P, D])).then_inc(weights_in, 16)
            with nc.allow_non_contiguous_dma(reason="bias columns, a few hundred elements"):
                sp.dma_start(gru_b[:, 0:3], L3_gnn_b_ih.rearrange("(c p) -> p c", p=P)).then_inc(weights_in, 16)
                sp.dma_start(gru_b[:, 3:6], L3_gnn_b_hh.rearrange("(c p) -> p c", p=P)).then_inc(weights_in, 16)
                sp.dma_start(ib_col[:, :], L3_gnn_i_b.rearrange("(p a) -> p a", a=1)).then_inc(weights_in, 16)
                sp.dma_start(jb_col[:, :], L3_gnn_j_b.rearrange("(p a) -> p a", a=1)).then_inc(weights_in, 16)

            sp.dma_start(X0[0:N, :], x).then_inc(x0_out, 16)
            sp.wait_ge(zeros_set, 1)
            sp.dma_start(X0[N:NPAD, :].rearrange("n f -> (n f)").rearrange("(p c) -> p c", p=P),
                         z[:, 0, 0:(NPAD - N) * D // P]).then_inc(x0_out, 16)
            src_empty = SRC_REC.rearrange("(l c) w -> l (c w)", c=NCH)
            for i in range(NCH // ZS):
                sp.dma_start(src_empty[:, i * ZS * RS:(i + 1) * ZS * RS], zero_src).then_inc(zeros_out, 16)
            sp.dma_start(DST_REC[E:E + P, :], empty_rec[:, :]).then_inc(empty_out, 16)
            sp.dma_start(DST_ATTR[E:E + P, :], z[:, 0, 0:DE]).then_inc(empty_out, 16)

            def pass_rows(d, left, loads, store, last=1):
                for slot, t in loads:
                    sp.dma_start(by_tile(slot[:, 0, :]), rows(t, 0)).then_inc(d.ld[0], 16)

                def step(j, par):
                    g = 2 * j + par
                    if not is_last(g):
                        wait(sp, left, g)
                        for slot, t in loads:
                            sp.dma_start(by_tile(slot[:, 1 - par, :]), rows(t, g + 1)).then_inc(d.ld[1 - par], 16)
                    if not isinstance(g, int) or g > 0:
                        sp.wait_ge(d.rows, g)
                        store(g - 1, 1 - par)
                groups(sp, step)
                sp.wait_ge(d.rows, NG)
                store(NG - 1, (NG - 1) % 2)
                for par in range(2):
                    sp.wait_ge(d.st[par], 16 * (NG // 2 + (1 - par) * last))

            def to_table(d, t):
                def store(g, par):
                    sp.dma_start(rows(t, g), by_tile(res[:, par, :])).then_inc(d.st[par], 16)
                return store

            sp.wait_ge(x0_out, 32)
            pass_rows(p_wx, p_wx.rows, [(xin, X0)], to_table(p_wx, WX))

            def chunks_out(t, numbers):
                sp.dma_start(t.rearrange("(p c) -> p c", p=P), numbers[:, :]).then_inc(off_out, 16)
            sp.wait_ge(off_ready, 1)
            chunks_out(SRC_OFF, tid_i)
            sp.wait_ge(off_ready, 2)
            for t, numbers in ((DST_OFF, tid_i), (DST_NODE, node), (DST_FIRST, first_i)):
                chunks_out(t, numbers)
            sp.wait_ge(off_out, 64)
            sp.dma_start(first_rec[:, :], DST_FIRST.rearrange("(a c) -> a c", a=1)).then_inc(nodes_in, 16)
            sp.dma_start(chunk_node, DST_NODE.rearrange("(a c) -> a c", a=1).to_broadcast([P, NCH])).then_inc(nodes_in, 16)

            attr = edge_attr_32[0:(P - 1) * EC, :].rearrange("(p e) f -> p e f", e=EC)
            attr_tail = edge_attr_32[(P - 1) * EC:E, :].rearrange("(p e) f -> p e f", p=1)

            def attr_turn(t, whole):
                for q in range(NQ):
                    wait(sp, sort_dma[q], t * 128)
                    c = t * U + q * 4
                    at = slice(c, c + 4) if isinstance(c, int) else bass.ds(c, 4)
                    for lo, hi in ((0, 112), (112, P - 1)):
                        sp.dma_start(rec[lo:hi, q * 4:q * 4 + 4, 0:DE], attr[lo:hi, at, :]).then_inc(sort_attr[q], 16)
                    if whole:
                        sp.dma_start(rec[P - 1:P, q * 4:q * 4 + 4, 0:DE], attr_tail[:, at, :]).then_inc(sort_attr[q], 16)

            sp.wait_ge(order_known, 1)
            sp.wait_ge(empty_out, 32)
            with sp.If(is_unsorted(mybir.EngineType.SP)):
                attr_turn(0, True)
                with sp.Fori(1, FULLTURNS) as t:
                    attr_turn(t, True)
                with sp.Fori(FULLTURNS, STURNS) as t:
                    attr_turn(t, False)
                for q in range(NQ):
                    sp.wait_ge(sort_dma[q], 128 * STURNS)
            with sp.Else():
                sp.dma_start(DST_ATTR[0:E, :].rearrange("(k e) f -> k (e f)", e=200),
                             edge_attr_32.rearrange("(k e) f -> k (e f)", e=200)).then_inc(sorted_out, 16)
                sp.wait_ge(pos_ready, 4)
                v = DST_REC[0:(P - 1) * EC, :].rearrange("(p e) w -> p e w", e=EC)
                for lo, hi in ((0, 112), (112, P - 1)):
                    sp.dma_start(v[lo:hi, :, :], d_rec[lo:hi, :, :]).then_inc(sorted_out, 16)
                sp.dma_start(DST_REC[(P - 1) * EC:E, :].rearrange("(p e) w -> p e w", p=1),
                             d_rec[P - 1:P, 0:ETAIL, :]).then_inc(sorted_out, 16)
                sp.wait_ge(sorted_out, 64)

            for u in range(U):
                sp.wait_ge(slot_dma[u], 16 * STURNS)
            sp.dma_start(aux[:, 0:RS * NCH], src_empty).then_inc(srcmeta_in, 16)
            sp.dma_start(tile_off[:, :], SRC_OFF.rearrange("(a c) -> a c", a=1)).then_inc(off_in, 16)

            sp.wait_ge(nodes_in, 32)

            def firsts(t):
                return loaded(mybir.EngineType.SP, first_rec[0:1, bass.ds(t * U, U)], U, E,
                              "the kernel bounds a chunk's first record by the number of edges")
            with sp.Fori(0, TURNS) as t:
                first = firsts(t)
                for u in range(U):
                    sp.dma_start(dstmeta[:, bass.ds(t * U + u, 1), :],
                                 DST_REC[bass.ds(first[u], P), :]).then_inc(records_in[u // 4], 16)

            pass_rows(p_l0, p_l0.var, [(xin, X0), (yin, WX)], to_table(p_l0, X1))

            sp.wait_ge(added, NCH + 1)
            sp.dma_start(tile_off[:, :], DST_OFF.rearrange("(a c) -> a c", a=1)).then_inc(off_in, 16)
            with sp.Fori(0, TURNS) as t:
                first = firsts(t)
                for q in range(NQ):
                    sp.wait_ge(summed[q], t + TURNS)
                    for u in range(q * 4, q * 4 + 4):
                        sp.dma_start(rec[:, u, 0:DE], DST_ATTR[bass.ds(first[u], P), :]).then_inc(attr_in[q], 16)

            pass_rows(p_l1, p_l1.var, [(xin, X1)], to_table(p_l1, X2))
            pass_rows(p_l2a, p_l2a.rows, [(xin, X2)], to_table(p_l2a, H1))
            pass_rows(p_l2b, p_l2b.var, [(xin, H1), (yin, X2)], to_table(p_l2b, X3))

            def t_store(n, g):
                for hh in range(2):
                    sp.wait_ge(t_rows[hh], n * NG + g + 1)
                    sp.dma_start(rows(TT, g)[:, hh * 2:hh * 2 + 2, :], by_tile(wide[:, hh, :], 2)).then_inc(t_out[hh], 16)

            sp.dma_start(by_tile(xin[:, 0, :]), rows(X3, 0)).then_inc(p_t.ld[0], 16)

            def t_step(j, par):
                g = 2 * j + par
                if not is_last(g):
                    wait(sp, p_t.turned, g)
                    sp.dma_start(by_tile(xin[:, 1 - par, :]), rows(X3, g + 1)).then_inc(p_t.ld[1 - par], 16)
                t_store(0, g)
            groups(sp, t_step)
            for n in (1, 2):
                with sp.Fori(0, NG) as g:
                    t_store(n, g)

            def to_out(g, par):
                if is_last(g):
                    for a in range(LAST_OUTS):
                        lo = g * GN + a * P
                        n = min(P, N - lo)
                        sp.dma_start(out[lo:lo + n, :], res[0:n, par, a * D:(a + 1) * D]).then_inc(p_fin.st[par], 16)
                else:
                    sp.dma_start(rows(out, g), by_tile(res[:, par, :])).then_inc(p_fin.st[par], 16)
            pass_rows(p_fin, p_fin.var, [(xin, X3)], to_out, LAST_OUTS)

        @block.gpsimd
        def _(pool):
            pool.memset(ones_f[:, :], 1.0)
            pool.memset(eps_col[:, :], EPS)
            pool.iota(iota_i[:, :], pattern=[[1, P]], base=0, channel_multiplier=0)
            pool.iota(chunk_i[:, :], pattern=[[1, IPC]], base=0, channel_multiplier=IPC).then_inc(pool_const, 1)
            pool.wait_ge(pool_const, 1)
            pool.affine_select(out=ident[:, :], in_=ones_f[:, :], compare_op=ALU.is_equal, fill=0.0, base=0,
                               pattern=[[-1, P]], channel_multiplier=1)
            pool.affine_select(out=before[:, :], in_=ones_f[:, :], compare_op=ALU.is_gt, fill=0.0, base=0,
                               pattern=[[1, P]], channel_multiplier=-1)
            pool.affine_select(out=deg_pick[:, :], in_=ones_f[0:DE + 1, 0:1], compare_op=ALU.is_equal, fill=0.0,
                               base=-DE, pattern=[[0, 1]], channel_multiplier=1).then_inc(const_ready, 1)
            pool.memset(z[:, 0, :], 0.0)
            pool.memset(zero_src, 0.0)
            pool.memset(empty_rec[:, :], 0.0).then_inc(pool_const, 1)
            pool.wait_ge(pool_const, 2)
            pool.memset(zero_src.rearrange("p (c w) -> p c w", w=RS)[:, :, 1:2], -1.0)
            pool.memset(empty_rec[:, 0:1], -1.0).then_inc(zeros_set, 1)

            def go(ready, n):
                pool.wait_ge(ready, n)
                pool.sem_inc(pool_seen, 1)

            go(zeros_out, 16 * (NCH // ZS))
            with pool.Fori(0, STURNS) as t:
                for q in range(NQ):
                    go(staged[q], t + 1)
                    for u in range(q * 4, q * 4 + 4):
                        pool.indirect_dma_start(
                            SRC_REC, bass.IndirectOffsetOnAxis(ap=stage[:, u:u + 1], axis=0), srec[:, u, :], None,
                            bounds_check=P * NCH - 1, oob_is_err=False).then_inc(slot_dma[u], 16)

            def by_dst(t, whole):
                for q in range(NQ):
                    go(sort_staged[q], t + 1)
                    go(sort_attr[q], t * 48 + 48 if whole else t * 32 + (16 * FULLTURNS + 32))
                    for u in range(q * 4, q * 4 + 4):
                        at = bass.IndirectOffsetOnAxis(ap=stage[:, u:u + 1], axis=0)
                        pool.indirect_dma_start(DST_REC, at, drec[:, u, :], None, bounds_check=E - 1,
                                                oob_is_err=False).then_inc(sort_dma[q], 16)
                        pool.indirect_dma_start(DST_ATTR, at, rec[:, u, 0:DE], None, bounds_check=E - 1,
                                                oob_is_err=False).then_inc(sort_dma[q], 16)
            go(order_known, 1)
            with pool.If(is_unsorted(mybir.EngineType.Pool)):
                with pool.Fori(0, FULLTURNS) as t:
                    by_dst(t, True)
                with pool.Fori(FULLTURNS, STURNS) as t:
                    by_dst(t, False)

            def gather(ph, table):
                with pool.Fori(0, TURNS) as t:
                    for q in range(NQ):
                        go(staged[q], STURNS + ph * TURNS + t + 1)
                        for u in range(q * 4, q * 4 + 4):
                            pool.indirect_dma_start(
                                msg[:, u, :], None, table, bass.IndirectOffsetOnAxis(ap=stage[:, u:u + 1], axis=0)
                            ).then_inc(slot_dma[u], 16)

            def table_out(d):
                for par in range(2):
                    pool.wait_ge(d.st[par], 16 * (NG // 2 + 1 - par))
                    pool.sem_inc(pool_seen, 1)

            for ph, (d, table) in enumerate(((p_wx, WX), (p_l0, X1), (p_l1, X2), (p_l2a, H1))):
                table_out(d)
                gather(ph, table)
            types = TT.rearrange("n (k f) -> (n k) f", k=KT)
            for n in range(3):
                for hh in range(2):
                    pool.wait_ge(t_out[hh], 16 * NG * (n + 1))
                    pool.sem_inc(pool_seen, 1)
                gather(4 + n, types)

        @block.scalar
        def _(act):
            for b in range(NW // 4):
                act.wait_ge(weights_turned, b + 1)
                n = 4 * P if b < NW // 4 - 1 else 3 * P + DE + 1
                act.activation(wT[:, 4 * b:4 * b + 4, :].rearrange("p a b -> p (a b)")[:, 0:n], bank[b][:, 0:n],
                               ACT.Copy).then_inc(weights_ready, 1)
            act.wait_ge(weights_turned, NW // 4 + 1)
            act.activation(c1[:, :], bank[5][:, 0:D], ACT.Copy)
            act.activation(c2[:, :], bank[5][0:DE + 1, D:2 * D], ACT.Copy).then_inc(weights_ready, 1)
            act.activation(gru_rz[:, 0:1], gru_b[:, 0:1], ACT.Identity, bias=gru_b[:, 3:4])
            act.activation(gru_rz[:, 1:2], gru_b[:, 1:2], ACT.Identity, bias=gru_b[:, 4:5]).then_inc(weights_ready, 1)

            def wx_step(j, par):
                g = 2 * j + par
                act.wait_ge(p_wx.turned, g + 1)
                act.activation(xT[:, par, :], bank[par][:, :], ACT.Copy).then_inc(p_wx.copied, 1)
                act.wait_ge(p_wx.prod, g + 1)
                wait(act, p_wx.st[par], 16 * j)
                act.activation(res[:, par, :], bank[2 + par][:, :], ACT.Copy).then_inc(p_wx.rows, 1)
            groups(act, wx_step)

            def stage_records(n, pos, fields, slot, records_left, ready):
                def turn(t):
                    for q in range(NQ):
                        records_left(t, q)
                        c = t * U + q * 4
                        act.activation(stage[:, q * 4:q * 4 + 4], cols(pos, c, 4), ACT.Copy)
                        act.activation(slot[:, q * 4:q * 4 + 4, :],
                                       fields[:, c:c + 4, :] if isinstance(c, int) else fields[:, bass.ds(c, 4), :],
                                       ACT.Copy).then_inc(ready[q], 1)
                act.wait_ge(pos_ready, 2 * n + 1)
                turn(0)
                with act.Fori(1, STURNS // 2) as t:
                    turn(t)
                act.wait_ge(pos_ready, 2 * n + 2)
                with act.Fori(STURNS // 2, STURNS) as t:
                    turn(t)

            def src_left(t, q):
                for u in range(q * 4, q * 4 + 4):
                    wait(act, slot_dma[u], t * 16)

            def dst_left(t, q):
                wait(act, sort_dma[q], t * 128)
            stage_records(0, s_pos, s_rec, srec, src_left, staged)
            act.wait_ge(order_known, 1)
            with act.If(is_unsorted(mybir.EngineType.Activation)):
                for u in range(U):
                    act.wait_ge(slot_dma[u], 16 * STURNS)
                stage_records(1, d_pos, d_rec, drec, dst_left, sort_staged)

            for q in range(NQ):
                act.wait_ge(records_in[q], 16 * NCH // NQ)
            for k, t in ((1, meta_w), (2, meta_src), (3, meta_row)):
                ins = act.activation(t[:, :], dstmeta[:, :, k], ACT.Copy)
            ins.then_inc(fields_ready, 1)

            def sqrt_step(d, g, par):
                act.wait_ge(d.var, g + 1)
                act.activation(std[:, par, :], mv[:, par, :, 1], ACT.Sqrt, bias=eps_col[:, 0:1]).then_inc(d.std, 1)

            def copies(d, g, par, features=False):
                wait(act, d.prod, g - 1)
                act.activation(accs[:, par, :], cols(acc, g * GN, GN), ACT.Copy)
                if features:
                    act.activation(auxs[0:DE + 1, par, :], cols(aux[0:DE + 1, :], g * GN, GN), ACT.Copy)
                act.wait_ge(d.turned, g + 1)
                act.activation(xT[:, par, :], bank[par][:, :], ACT.Copy).then_inc(d.copied, 1)

            def pass_copies(d, ph, features=False, roots=True):
                act.wait_ge(added, (ph + 1) * (NCH + 1))
                if features:
                    act.wait_ge(feat_added, NCH + 1)
                copies(d, 0, 0, features)

                def step(j, par):
                    g = 2 * j + par
                    if not is_last(g):
                        copies(d, g + 1, 1 - par, features)
                    if roots:
                        sqrt_step(d, g, par)
                groups(act, step)

            groups(act, lambda j, par: sqrt_step(p_l0, 2 * j + par, par))
            pass_copies(p_l1, 1, features=True)
            pass_copies(p_l2a, 2, roots=False)
            pass_copies(p_l2b, 3)

            def state_step(j, par):
                g = 2 * j + par
                act.wait_ge(p_t.turned, g + 1)
                act.activation(cols(aux, g * GN, GN), bank[par][:, :], ACT.Copy)
                wait(act, t_prod[1], g - 1)
                act.activation(auxs[:, par, :], bank[par][:, :], ACT.Copy).then_inc(p_t.copied, 1)
            groups(act, state_step)

            for n in range(3):
                def gate_step(j, par):
                    g = 2 * j + par
                    act.wait_ge(gate_prod, n * NG + g + 1)
                    act.activation(xT[:, par, :], bank[0][:, :], ACT.Sigmoid, bias=gru_rz[:, 0:1])
                    act.activation(accs[:, par, :], bank[1][:, :], ACT.Sigmoid, bias=gru_rz[:, 1:2]).then_inc(gate_rz, 1)
                    act.wait_ge(gate_pre, n * NG + g + 1)
                    act.activation(yin[:, par, :], y[:, :], ACT.Tanh, bias=gru_b[:, 2:3]).then_inc(gate_n, 1)
                    if n < 2:
                        act.wait_ge(h_ready, n * NG + g + 1)
                        act.wait_ge(t_prod[1], (n + 1) * NG + g - 1)
                        act.activation(auxs[:, par, :], cols(aux, g * GN, GN), ACT.Copy).then_inc(h_copied, 1)
                groups(act, gate_step)

            def fin_copy(g, par):
                wait(act, p_fin.prod, g - 1)
                act.wait_ge(p_fin.turned, g + 1)
                act.activation(xT[:, par, :], bank[par][:, :], ACT.Copy).then_inc(p_fin.copied, 1)
            fin_copy(0, 0)

            def fin_step(j, par):
                g = 2 * j + par
                act.wait_ge(p_fin.prod, g + 1)
                act.activation(yin[:, par, :], bank[2][:, :], ACT.Sigmoid, bias=ib_col[:, 0:1]).then_inc(gate_rz, 1)
                if not isinstance(g, int) or g > 0:
                    sqrt_step(p_fin, g - 1, 1 - par)
                if not is_last(g):
                    fin_copy(g + 1, 1 - par)
            groups(act, fin_step)
            sqrt_step(p_fin, NG - 1, (NG - 1) % 2)

        @block.tensor
        def _(pe):
            pe.wait_ge(const_ready, 1)
            pe.wait_ge(weights_in, 16 * WEIGHT_DMAS)
            for i in range(NW):
                rows_ = P if i < NW - 1 else DE + 1
                mm = pe.transpose(bank[i // 4][:, (i % 4) * P:(i % 4) * P + rows_], ring[0:rows_, i, :],
                                  ident[0:rows_, 0:rows_])
                if i % 4 == 3:
                    mm.then_inc(weights_turned, 1)
            pe.wait_ge(weights_ready, NW // 4)
            pe.matmul(bank[5][:, 0:D], wT[:, W_1A, :], w2b[:, :], start=True, stop=True)
            pe.matmul(bank[5][0:DE + 1, D:2 * D], wT[:, W_1B, 0:DE + 1], w2b[:, :], start=True,
                      stop=True).then_inc(weights_turned, 1)

            def sort_sums(n):
                pe.wait_ge(hist_ready, n + 1)
                pe.matmul(bank[6][:, 0:NT], before[:, :], hist[:, :], start=True, stop=True)
                pe.matmul(bank[6][:, P:P + NT], ones_f[:, :], hist[:, :], start=True, stop=True).then_inc(base_sums, 1)
            sort_sums(0)

            def ahead(d, prod, loads=1):
                turn_rows(d, 0, 0, loads)

                def step(j, par):
                    g = 2 * j + par
                    if not is_last(g):
                        wait(pe, d.copied, g)
                        turn_rows(d, j + par, 1 - par, loads)
                    pe.wait_ge(d.copied, g + 1)
                    prod(g, par)
                groups(pe, step)

            def turn_rows(d, j, par, loads=1):
                pe.wait_ge(d.ld[par], (j + 1) * 16 * loads)
                for a in range(A):
                    mm = pe.transpose(bank[par][:, a * P:(a + 1) * P], xin[:, par, a * D:(a + 1) * D], ident[:, :])
                mm.then_inc(d.turned, 1)

            pe.wait_ge(weights_ready, NW // 4 + 2)

            def wx_step(j, par):
                g = 2 * j + par
                turn_rows(p_wx, j, par)
                pe.wait_ge(p_wx.copied, g + 1)
                wait(pe, p_wx.rows, g)
                for a in range(A):
                    o = bank[2 + par][:, a * D:(a + 1) * D]
                    pe.matmul(o, xT[:, par, a * P:(a + 1) * P], wT[:, W_0, :], start=True, stop=False)
                    mm = pe.matmul(o, ones_f[0:1, :], b0_row[:, :], start=False, stop=True)
                mm.then_inc(p_wx.prod, 1)
            groups(pe, wx_step)
            pe.wait_ge(falls_ready, 1)
            pe.matmul(bank[6][0:1, 2 * P:2 * P + 1], falls[:, :], ones_f[:, 0:1], start=True,
                      stop=True).then_inc(falls_summed, 1)
            sort_sums(1)

            def sums(ph, by_node=False, features=False):
                with pe.Fori(0, TURNS) as t:
                    for q in range(NQ):
                        pe.wait_ge(hot_ready[q], ph * TURNS + t + 1)
                        if features:
                            pe.wait_ge(attr_in[q], (t + 1) * 64)
                        for u in range(q * 4, q * 4 + 4):
                            k = u % 4
                            pe.wait_ge(slot_dma[u], (STURNS + ph * TURNS + t + 1) * 16)
                            lhs, rhs = (hot, msg) if by_node else (msg, hot)
                            if features:
                                pe.matmul(bank[4 + q][0:DE + 1, k * P:(k + 1) * P], rec[:, u, 0:DE + 1], hot[:, u, :],
                                          start=True, stop=True)
                            mm = pe.matmul(bank[q][:, k * P:(k + 1) * P], lhs[:, u, :], rhs[:, u, :],
                                           start=True, stop=True)
                        mm.then_inc(summed[q], 1)
                pe.wait_ge(added, (ph + 1) * (NCH + 1))
                if features:
                    pe.wait_ge(feat_added, NCH + 1)

            sums(0, by_node=True)
            sums(1, features=True)

            def l1_prod(g, par):
                pe.wait_ge(p_l1.free, g + 1)
                for a in range(A):
                    o = bank[2 + par][:, a * D:(a + 1) * D]
                    pe.matmul(o, xT[:, par, a * P:(a + 1) * P], w2a[:, :], start=True, stop=False)
                    pe.matmul(o, accs[:, par, a * P:(a + 1) * P], c1[:, :], start=False, stop=False)
                    pe.matmul(o, auxs[0:DE + 1, par, a * P:(a + 1) * P], c2[:, :], start=False, stop=True)
                    mm = pe.matmul(bank[4 + par][:, a:a + 1], auxs[0:DE + 1, par, a * P:(a + 1) * P], deg_pick[:, :],
                                   start=True, stop=True)
                mm.then_inc(p_l1.prod, 1)
            ahead(p_l1, l1_prod)

            def l2_steps(d, wl, wr, loads):
                def prod(g, par):
                    pe.wait_ge(d.free, g + 1)
                    for a in range(A):
                        pe.matmul(bank[2 + par][:, a * D:(a + 1) * D], accs[:, par, a * P:(a + 1) * P], wT[:, wl, :],
                                  start=True, stop=True)
                        mm = pe.matmul(bank[4 + par][:, a * D:(a + 1) * D], xT[:, par, a * P:(a + 1) * P], wT[:, wr, :],
                                       start=True, stop=True)
                    mm.then_inc(d.prod, 1)
                ahead(d, prod, loads)
            sums(2)
            l2_steps(p_l2a, W_1L, W_1R, 1)
            sums(3)
            l2_steps(p_l2b, W_2L, W_2R, 2)

            def types(n, g, par):
                for a in range(A):
                    if a % 2 == 0:
                        wait(pe, t_rows[a // 2], n * NG + g)
                    mm = pe.matmul(bank[2 + a][:, :], auxs[:, par, a * P:(a + 1) * P],
                                   wT[:, W_ET:W_ET + KT, :].rearrange("p k f -> p (k f)"), start=True, stop=True)
                    if a % 2:
                        mm.then_inc(t_prod[a // 2], 1)
            ahead(p_t, lambda g, par: types(0, g, par))

            for n in range(3):
                sums(4 + n)

                def gate_step(j, par):
                    g = 2 * j + par
                    i = n * NG + g
                    a, h = cols(acc, g * GN, GN), cols(aux, g * GN, GN)
                    wait(pe, gate_rz, i)
                    for c in range(2):
                        pe.matmul(bank[c][:, :], wT[:, W_IH + c, :], a, start=True, stop=False)
                        mm = pe.matmul(bank[c][:, :], wT[:, W_HH + c, :], h, start=False, stop=True)
                    mm.then_inc(gate_prod, 1)
                    wait(pe, gate_pre, i)
                    pe.matmul(bank[6][:, :], wT[:, W_IH + 2, :], a, start=True, stop=True)
                    pe.matmul(bank[7][:, :], wT[:, W_HH + 2, :], h, start=True, stop=True).then_inc(gate_nprod, 1)
                    if n < 2 and (not isinstance(g, int) or g > 0):
                        pe.wait_ge(h_copied, i)
                        types(n + 1, g - 1, 1 - par)
                groups(pe, gate_step)
                if n < 2:
                    pe.wait_ge(h_copied, (n + 1) * NG)
                    types(n + 1, NG - 1, (NG - 1) % 2)

            pe.wait_ge(h_ready, 3 * NG)

            def turn_out(g, par):
                pe.wait_ge(p_fin.free, g + 1)
                wait(pe, p_fin.var, g - 1)
                for a in range(A):
                    mm = pe.transpose(bank[4 + par][:, a * P:(a + 1) * P], accs[:, par, a * P:(a + 1) * P], ident[:, :])
                mm.then_inc(out_turned, 1)

            turn_rows(p_fin, 0, 0)

            def fin_step(j, par):
                g = 2 * j + par
                pe.wait_ge(p_fin.copied, g + 1)
                wait(pe, p_fin.free, g)
                h = cols(aux, g * GN, GN)
                pe.matmul(bank[2][:, :], wT[:, W_I, :], h, start=True, stop=False)
                pe.matmul(bank[2][:, :], wT[:, W_I + 1, :], xT[:, par, :], start=False, stop=True)
                pe.matmul(bank[3][:, :], wT[:, W_J, :], h, start=True, stop=True).then_inc(p_fin.prod, 1)
                if not isinstance(g, int) or g > 0:
                    turn_out(g - 1, 1 - par)
                if not is_last(g):
                    turn_rows(p_fin, j + par, 1 - par)
            groups(pe, fin_step)
            turn_out(NG - 1, (NG - 1) % 2)

        @block.vector
        def _(v):
            class Chain:
                base = per = k = 0
                turn = 0

                def link(self, ins):
                    self.k += 1
                    ins.then_inc(chain, 1)
                    v.wait_ge(chain, self.turn * self.per + (self.base + self.k))

                def loop(self, turn, per, first=0):
                    self.turn, self.per, self.k = turn, per, 0
                    self.base -= first * per

                def end(self, turns=1, first=0):
                    assert not self.per or self.k == self.per, (self.k, self.per)
                    self.base += (turns + first) * self.per if self.per else self.k
                    self.turn = self.per = self.k = 0
            ch = Chain()
            link = ch.link

            def linked(step, per):
                for j in range(FIRST):
                    step(j, 0)
                    step(j, 1)
                ch.end()
                with v.Fori(FIRST, NG // 2) as j:
                    ch.loop(j, per, first=FIRST)
                    step(j, 0)
                    step(j, 1)
                ch.end(NG // 2 - FIRST, first=FIRST)
                step(NG // 2, 0)
                ch.end()

            v.memset(s_key.bitcast(I32)[96:P, ETAIL:EC], -1).then_inc(tails_set, 1)
            v.memset(d_key.bitcast(I32)[96:P, ETAIL:EC], -1).then_inc(tails_set, 1)
            v.memset(d_pos.bitcast(I32)[96:P, ETAIL - 1:EC], NPAD).then_inc(tails_set, 1)
            v.memset(meta_w[96:P, ETAIL:EC], 0.0).then_inc(tails_set, 1)
            v.memset(meta_low[:, 0:EC].bitcast(I32)[96:P, ETAIL:EC], 0).then_inc(tails_set, 1)
            v.wait_ge(const_ready, 1)
            v.tensor_copy(iota_f[:, :], iota_i[:, :])
            link(v.tensor_copy(chunk_f[:, :], chunk_i[:, :]))

            def places(key, tile, low):
                a = s_mask.bitcast(I32)
                link(v.tensor_scalar(a, key, 7, None, ALU.arith_shift_right))
                link(v.tensor_copy(tile, a))
                if low is not None:
                    link(v.tensor_scalar(a, key, P - 1, None, ALU.bitwise_and))
                    link(v.tensor_copy(low, a))

            HC = EC // 2

            def count(tile):
                ch.end()
                with v.Fori(0, NT) as t:
                    ch.loop(t, 2)
                    for h, hist_h in enumerate((hist0, hist)):
                        link(v.tensor_scalar(s_mask[:, h * HC:(h + 1) * HC], tile[:, h * HC:(h + 1) * HC],
                                             iota_f[:, bass.ds(t, 1)], 0.0, ALU.is_equal, ALU.add,
                                             accum_out=hist_h[:, bass.ds(t, 1)]))
                ch.end(NT)
                v.tensor_tensor(hist[:, :], hist[:, :], hist0[:, :], ALU.add).then_inc(hist_ready, 1)

            def starts(n):
                v.wait_ge(base_sums, n + 1)
                link(v.tensor_scalar(cnt_i[:, :], bank[6][:, P:P + NT], float(P - 1), None, ALU.add))
                link(v.tensor_scalar(cnt_i[:, :], cnt_i[:, :], 7, None, ALU.arith_shift_right))
                link(v.tensor_copy(cnt_f[:, :], cnt_i[:, :]))
                link(v.tensor_tensor_scan(cum[:, :], cnt_f[:, :], cnt_f[:, :], 0.0, ALU.add, ALU.max))
                if n == 0:
                    link(v.tensor_tensor(spare[:, :], cum[:, :], cnt_f[:, :], ALU.subtract))
                    link(v.scalar_tensor_tensor(out=base[:, :], in0=spare[:, :], scalar=float(P), in1=bank[6][:, 0:NT],
                                                op0=ALU.mult, op1=ALU.add))
                else:
                    link(v.scalar_tensor_tensor(out=pads[:, :], in0=cnt_f[:, :], scalar=float(P),
                                                in1=bank[6][:, P:P + NT], op0=ALU.mult, op1=ALU.subtract))
                    link(v.tensor_copy(cnt_f[:, :], bank[6][:, P:P + NT]))
                    link(v.tensor_tensor_scan(spare[:, :], cnt_f[:, :], cnt_f[:, :], 0.0, ALU.add, ALU.max))
                    link(v.tensor_tensor(spare[:, :], spare[:, :], cnt_f[:, :], ALU.subtract))
                    link(v.tensor_tensor(base[:, :], spare[:, :], bank[6][:, 0:NT], ALU.add))

            def chunk_tiles(n):
                for c in range(IPC):
                    link(v.tensor_scalar(spare[:, :], cum[:, :], chunk_f[:, c:c + 1], 0.0, ALU.is_le, ALU.add,
                                         accum_out=tid[:, c:c + 1]))
                    if n:
                        link(v.tensor_tensor(spare[:, :], spare[:, :], pads[:, :], ALU.mult))
                        link(v.tensor_scalar(spare[:, :], spare[:, :], 0.0, 0.0, ALU.add, ALU.add,
                                             accum_out=shift[:, c:c + 1]))
                if n:
                    link(v.scalar_tensor_tensor(out=shift[:, :], in0=chunk_f[:, :], scalar=float(P), in1=shift[:, :],
                                                op0=ALU.mult, op1=ALU.subtract))
                    v.tensor_scalar(first_i[:, :], shift[:, :], float(E), None, ALU.min)
                    v.tensor_scalar(node[:, :], tid[:, :], float(NT - 1), float(P), ALU.min, ALU.mult)
                    v.wait_ge(off_out, 16)
                v.tensor_scalar(tid_i[:, :], tid[:, :], float(NT - 1), float(P), ALU.min, ALU.mult).then_inc(off_ready, 1)

            def positions(n, tile, pos_all):
                link(v.memset(pos_all, FAR))
                for h in range(2):
                    lo = h * HC
                    pos, scan = pos_all[:, lo:lo + HC], s_scan[:, lo:lo + HC]
                    key, mask = tile[:, lo:lo + HC], s_mask.bitcast(BF16)[:, lo:lo + HC]
                    if h:
                        link(v.tensor_tensor(base[:, :], base[:, :], hist0[:, :], ALU.add))
                    ch.end()
                    with v.Fori(0, NT) as t:
                        ch.loop(t, 3)
                        link(v.tensor_scalar(mask, key, iota_f[:, bass.ds(t, 1)], None, ALU.is_equal))
                        link(v.tensor_tensor_scan(scan, mask, mask, base[:, bass.ds(t, 1)], ALU.add, ALU.max))
                        v.sem_inc(vec_seen, 1)
                        link(v.copy_predicated(pos, mask.bitcast(U16), scan))
                    ch.end(NT)
                    if n:
                        v.tensor_scalar(pos, pos, -1.0, None, ALU.add).then_inc(pos_ready, 1)
                        continue
                    a, b = s_mask.bitcast(I32)[:, lo:lo + HC], s_scan.bitcast(I32)[:, lo:lo + HC]
                    link(v.tensor_scalar(a, pos, -1.0, None, ALU.add))
                    link(v.tensor_scalar(b, a, P - 1, None, ALU.bitwise_and))
                    link(v.tensor_scalar(a, a, 7, None, ALU.arith_shift_right))
                    v.scalar_tensor_tensor(out=pos, in0=b, scalar=float(NCH), in1=a, op0=ALU.mult,
                                           op1=ALU.add).then_inc(pos_ready, 1)
                    v.wait_ge(pos_ready, h + 1)

            si, di = s_key.bitcast(I32), d_key.bitcast(I32)
            v.wait_ge(keys_in, 16 * 12)
            places(si, s_tile, s_rec[:, :, 1])
            count(s_tile)
            v.tensor_copy(s_rec[:, :, 0], di)
            link(v.tensor_tensor(s_mask, si, di, ALU.not_equal))
            link(v.tensor_tensor(s_scan, meta_w[:, 0:EC], meta_w[:, 0:EC], ALU.mult))
            link(v.tensor_tensor(s_rec[:, :, 2], s_mask, s_scan, ALU.mult))
            starts(0)
            positions(0, s_tile, s_pos)
            chunk_tiles(0)
            v.wait_ge(next_in, 48)
            link(v.tensor_tensor(s_mask, di, d_pos.bitcast(I32), ALU.is_gt))
            v.tensor_scalar(s_scan, s_mask, 0.0, 0.0, ALU.add, ALU.add, accum_out=falls[:, :]).then_inc(falls_ready, 1)
            v.wait_ge(falls_summed, 1)
            v.tensor_scalar(unsorted[:, :], bank[6][0:1, 2 * P:2 * P + 1], 1.0, None, ALU.min).then_inc(order_known, 1)
            v.tensor_copy(d_rec[:, :, 0], di)
            v.tensor_copy(d_rec[:, :, 1], meta_w[:, 0:EC])
            v.tensor_copy(d_rec[:, :, 2], si)
            v.scalar_tensor_tensor(out=d_rec[:, :, 3], in0=si, scalar=float(KT), in1=meta_low[:, 0:EC].bitcast(I32),
                                   op0=ALU.mult, op1=ALU.add)
            places(di, d_tile, None)
            count(d_tile)
            starts(1)
            positions(1, d_tile, d_pos)
            chunk_tiles(1)
            ch.end()

            def gather_steps(ph, index, low, weight, features=False):
                def add(t, u, off):
                    v.wait_ge(added, t * U + (ph * (NCH + 1) + u + 1))
                    into = acc[:, bass.ds(off, P)]
                    k = u % 4
                    ins = v.tensor_tensor(into, into, bank[u // 4][:, k * P:(k + 1) * P], ALU.add)
                    ins.then_inc(added, 1)
                    if features:
                        v.wait_ge(feat_added, t * U + (u + 1))
                        into = aux[0:DE + 1, bass.ds(off, P)]
                        v.tensor_tensor(into, into, bank[4 + u // 4][0:DE + 1, k * P:(k + 1) * P],
                                        ALU.add).then_inc(feat_added, 1)

                def offsets(t):
                    return loaded(mybir.EngineType.DVE, cols(tile_off, t * U, U), U, (NT - 1) * P,
                                  "the kernel writes 128 times a tile number, at most NT - 1")

                def turn(t, first=False):
                    if not first:
                        off = offsets(t - 1)
                    for q in range(NQ):
                        if not first:
                            v.wait_ge(summed[q], ph * TURNS + t)
                        c = t * U + q * 4
                        v.tensor_copy(stage[:, q * 4:q * 4 + 4], index(c, 4)).then_inc(staged[q], 1)
                        for u in range(q * 4, q * 4 + 4):
                            if not first:
                                add(t - 1, u, off[u])
                            ins = v.tensor_scalar(hot[:, u, :], iota_f[:, :], low(c + u % 4),
                                                  weight(c + u % 4) if weight else None, ALU.is_equal,
                                                  ALU.mult if weight else ALU.bypass)
                        ins.then_inc(hot_ready[q], 1)

                turn(0, first=True)
                v.memset(acc[:, :], 0.0).then_inc(added, 1)
                if features:
                    v.memset(aux[0:DE + 1, :], 0.0).then_inc(feat_added, 1)
                with v.Fori(1, TURNS) as t:
                    turn(t)
                off = offsets(TURNS - 1)
                for q in range(NQ):
                    v.wait_ge(summed[q], (ph + 1) * TURNS)
                    for u in range(q * 4, q * 4 + 4):
                        add(TURNS - 1, u, off[u])
                v.wait_ge(added, (ph + 1) * (NCH + 1))
                if features:
                    v.wait_ge(feat_added, NCH + 1)

            def moments(d, par):
                for a in range(A):
                    ins = v.bn_stats(stats[:, a, :], z[:, par, a * D:(a + 1) * D])
                link(ins)
                v.sem_inc(vec_seen, 1)
                for a in range(A):
                    ins = v.bn_aggr(mv[:, par, a, :], stats[:, a, :])
                ins.then_inc(d.var, 1)

            def norm(d, g, j, par):
                v.wait_ge(d.std, g + 1)
                link(v.reciprocal(rstd[:, par, :], std[:, par, :]))
                wait(v, d.st[par], j * 16)
                for a in range(A):
                    ins = v.tensor_scalar(res[:, par, a * D:(a + 1) * D], z[:, par, a * D:(a + 1) * D],
                                          mv[:, par, a, 0:1], rstd[:, par, a:a + 1], ALU.subtract, ALU.mult)
                ins.then_inc(d.rows, 1)

            def normed(d, rows_of, per):
                def step(j, par):
                    g = 2 * j + par
                    wait(v, d.rows, g - 1)
                    rows_of(g, j, par)
                    moments(d, par)
                    if not isinstance(g, int) or g > 0:
                        norm(d, g - 1, j - 1 + par, 1 - par)
                linked(step, 2 * per)
                norm(d, NG - 1, (NG - 1) // 2, (NG - 1) % 2)
                ch.end()

            v.wait_ge(srcmeta_in, 16)
            v.wait_ge(off_in, 16)
            gather_steps(0, lambda c, n: srcmeta[:, c:c + n, 0] if isinstance(c, int) else srcmeta[:, bass.ds(c, n), 0],
                         lambda c: cols(aux[:, 0:RS * NCH], c * RS + 1, 1),
                         lambda c: cols(aux[:, 0:RS * NCH], c * RS + 2, 1))

            def l0_rows(g, j, par):
                v.wait_ge(p_l0.ld[par], (j + 1) * 32)
                link(v.tensor_tensor(z[:, par, :], yin[:, par, :], cols(acc, g * GN, GN), ALU.mult))
                link(v.tensor_tensor(z[:, par, :], z[:, par, :], xin[:, par, :], ALU.add))
            normed(p_l0, l0_rows, 4)

            v.wait_ge(fields_ready, 1)
            v.wait_ge(off_in, 32)
            v.memset(rec[:, :, DE:DE + 1], 1.0)
            link(v.tensor_tensor(meta_low[:, :], dstmeta[:, :, 0], chunk_node, ALU.subtract))
            src_of = lambda c, n: cols(meta_src, c, n)
            low_of = lambda c: cols(meta_low, c, 1)
            weight_of = lambda c: cols(meta_w, c, 1)
            gather_steps(1, src_of, low_of, None, features=True)
            v.sem_inc(p_l1.free, 2)

            def l1_rows(g, j, par):
                dg = cnt_f[:, par * 2 * A:(par + 1) * 2 * A]
                v.wait_ge(p_l1.prod, g + 1)
                v.tensor_scalar(dg[:, 0:A], bank[4 + par][:, 0:A], 1.0, None, ALU.max)
                link(v.tensor_tensor(z[:, par, :], bank[2 + par][:, :], xin[:, par, :], ALU.add))
                v.sem_inc(p_l1.free, 1)
                v.tensor_tensor(dg[:, A:2 * A], dg[:, 0:A], dg[:, 0:A], ALU.mult)
                link(v.tensor_tensor(z[:, par, :], z[:, par, :], b2_all[:, :], ALU.add))
                v.reciprocal(cols(rdeg, g * A, A), dg[:, A:2 * A])
            normed(p_l1, l1_rows, 4)

            def combine(d, par, g):
                for a in range(A):
                    ins = v.tensor_scalar(z[:, par, a * D:(a + 1) * D], bank[2 + par][:, a * D:(a + 1) * D],
                                          cols(rdeg, g * A + a, 1), None, ALU.mult)
                link(ins)
                link(v.tensor_tensor(z[:, par, :], z[:, par, :], bank[4 + par][:, :], ALU.add))
                v.sem_inc(d.free, 1)

            gather_steps(2, src_of, low_of, weight_of)
            v.sem_inc(p_l2a.free, 2)

            def l2a_step(j, par):
                g = 2 * j + par
                v.wait_ge(p_l2a.prod, g + 1)
                wait(v, p_l2a.rows, g - 1)
                combine(p_l2a, par, g)
                wait(v, p_l2a.st[par], j * 16)
                v.tensor_scalar(res[:, par, :], z[:, par, :], 0.0, None, ALU.max).then_inc(p_l2a.rows, 1)
            linked(l2a_step, 4)
            gather_steps(3, src_of, low_of, weight_of)
            v.sem_inc(p_l2b.free, 2)

            def l2b_rows(g, j, par):
                v.wait_ge(p_l2b.prod, g + 1)
                combine(p_l2b, par, g)
                link(v.tensor_tensor(z[:, par, :], z[:, par, :], yin[:, par, :], ALU.add))
            normed(p_l2b, l2b_rows, 5)

            def t_add(n, g):
                for hh in range(2):
                    v.wait_ge(t_prod[hh], n * NG + g + 1)
                    wait(v, t_out[hh], (n * NG + g) * 16)
                    for a in range(2):
                        ins = v.tensor_tensor(wide[:, hh, a * KT * D:(a + 1) * KT * D], bank[2 + 2 * hh + a][:, :],
                                              bet_all[:, :], ALU.add)
                    ins.then_inc(t_rows[hh], 1)
            groups(v, lambda j, par: t_add(0, 2 * j + par))

            for n in range(3):
                gather_steps(4 + n, lambda c, k: cols(meta_row, c, k), low_of, None)

                def gru_step(j, par):
                    g = 2 * j + par
                    i = n * NG + g
                    h = cols(aux, g * GN, GN)
                    v.wait_ge(gate_rz, i + 1)
                    v.wait_ge(gate_nprod, i + 1)
                    wait(v, h_ready, i)
                    link(v.scalar_tensor_tensor(out=z[:, 0, :], in0=bank[7][:, :], scalar=gru_b[:, 5:6],
                                                in1=xT[:, par, :], op0=ALU.add, op1=ALU.mult))
                    v.tensor_tensor(y[:, :], z[:, 0, :], bank[6][:, :], ALU.add).then_inc(gate_pre, 1)
                    if n < 2 and (not isinstance(g, int) or g > 0):
                        t_add(n + 1, g - 1)
                    v.wait_ge(gate_n, i + 1)
                    link(v.tensor_tensor(z[:, 1, :], h, yin[:, par, :], ALU.subtract))
                    link(v.tensor_tensor(z[:, 1, :], z[:, 1, :], accs[:, par, :], ALU.mult))
                    v.tensor_tensor(h, z[:, 1, :], yin[:, par, :], ALU.add).then_inc(h_ready, 1)
                linked(gru_step, 6)
                if n < 2:
                    t_add(n + 1, NG - 1)

            v.wait_ge(h_ready, 3 * NG)

            def fin_norm(g, j, par):
                v.wait_ge(out_turned, g + 1)
                wait(v, p_fin.rows, g)
                link(v.tensor_tensor(z[:, par, :], bank[4 + par][:, :], xin[:, par, :], ALU.add))
                moments(p_fin, par)
                norm(p_fin, g, j, par)

            def fin_step(j, par):
                g = 2 * j + par
                v.wait_ge(gate_rz, 3 * NG + g + 1)
                v.scalar_tensor_tensor(out=accs[:, par, :], in0=bank[3][:, :], scalar=jb_col[:, 0:1],
                                       in1=yin[:, par, :], op0=ALU.add, op1=ALU.mult).then_inc(p_fin.free, 1)
                if not isinstance(g, int) or g > 0:
                    fin_norm(g - 1, j - 1 + par, 1 - par)
            linked(fin_step, 6)
            fin_norm(NG - 1, (NG - 1) // 2, (NG - 1) % 2)


_INS = ['x', 'src', 'dst', 'edge_attr_32', 'edge_type_4', 'edge_weight', 'L0_gnn_W', 'L0_gnn_b', 'L1_gnn_u', 'L1_gnn_W1',
        'L1_gnn_b1', 'L1_gnn_W2', 'L1_gnn_b2', 'L2_gnn_W1l', 'L2_gnn_W1r', 'L2_gnn_W2l', 'L2_gnn_W2r', 'L3_gnn_W_et',
        'L3_gnn_b_et', 'L3_gnn_W_ih', 'L3_gnn_b_ih', 'L3_gnn_W_hh', 'L3_gnn_b_hh', 'L3_gnn_i_w', 'L3_gnn_i_b',
        'L3_gnn_j_w', 'L3_gnn_j_b']


def kernel(**inputs):
    import numpy as _np
    import concourse.bacc as _bacc
    from concourse import mybir as _mybir
    from concourse.bass_utils import run_bass_kernel_spmd as _run

    nc = _bacc.Bacc("TRN2", target_bir_lowering=False, num_devices=1)
    arrays, args = {}, []
    for name in _INS:
        a = _np.ascontiguousarray(inputs[name])
        arrays[f"in_{name}"] = a
        args.append(nc.dram_tensor(f"in_{name}", a.shape, _mybir.dt.from_np(a.dtype), kind="ExternalInput").ap())
    o = nc.dram_tensor("out_0", (N, D), F32, kind="ExternalOutput").ap()
    build(nc, *args, o)
    r = _run(nc, [arrays], core_ids=[0])
    return r.results[0]["out_0"]
```
